# Optimizing a Trainium2 kernel written in Bass

```python
import numpy as np
import jax
import jax.numpy as jnp

def _softmax(x, axis=-1):
    return jax.nn.softmax(x, axis=axis)

def _gelu(x):
    return jax.nn.gelu(x, approximate=True)

def _silu(x):
    return jax.nn.silu(x)

def _sigmoid(x):
    return jax.nn.sigmoid(x)

def _layernorm(x, axis=-1, eps=1e-05):
    m = jnp.mean(x, axis=axis, keepdims=True)
    v = jnp.var(x, axis=axis, keepdims=True)
    return (x - m) / jnp.sqrt(v + eps)

def _scatter_add(tgt, idx, src, axis=0):
    return tgt.at[idx].add(src)

def _segment_sum(src, seg, n):
    return jax.ops.segment_sum(src, seg, n)
kernel_name = 'mk_seq_postln_d1_jaxref_r4_12b041'

def setup_inputs(seed: int=0):
    np.random.seed(seed)
    _w = jnp.asarray

    def _L0_attn_setup():
        import jax, jax.numpy as jnp
        import numpy as np
        WIDTH = 512
        NUM_HEADS = 16
        HEAD_DIM = WIDTH // NUM_HEADS
        ROPE_DIMS = HEAD_DIM // 2
        WINDOW = 128
        ROPE_BASE = 10000.0
        NEG_INF = -1000000000.0

        def apply_rope(x, dims, offset=0, base=ROPE_BASE):
            L = x.shape[2]
            half = dims // 2
            pos = (offset + jnp.arange(L)).astype(x.dtype)
            inv_freq = jnp.exp(-jnp.log(jnp.asarray(base, x.dtype)) * (jnp.arange(0, dims, 2).astype(x.dtype) / dims))
            theta = pos[:, None] * inv_freq[None, :]
            cos = jnp.cos(theta)[None, None]
            sin = jnp.sin(theta)[None, None]
            x1 = x[..., :half]
            x2 = x[..., half:dims]
            rest = x[..., dims:]
            rx1 = x1 * cos - x2 * sin
            rx2 = x1 * sin + x2 * cos
            return jnp.concatenate([rx1, rx2, rest], axis=-1)
        key = jax.random.key(seed)
        ks = jax.random.split(key, 6)
        B, L, D, hd = (2, 512, WIDTH, HEAD_DIM)
        x = jax.random.normal(ks[0], (B, L, D), dtype=jnp.float32)
        Wq = jax.random.normal(ks[1], (D, D), dtype=jnp.float32) * 0.02
        Wk = jax.random.normal(ks[2], (D, hd), dtype=jnp.float32) * 0.02
        Wv = jax.random.normal(ks[3], (D, hd), dtype=jnp.float32) * 0.02
        Wo = jax.random.normal(ks[4], (D, D), dtype=jnp.float32) * 0.02
        bo = jax.random.normal(ks[5], (D,), dtype=jnp.float32) * 0.02
        return {'x': x, 'Wq': Wq, 'Wk': Wk, 'Wv': Wv, 'Wo': Wo, 'bo': bo}
    _L0_attn_in = _L0_attn_setup()

    def _L0_ffn_setup():
        import jax, jax.numpy as jnp
        import numpy as np
        B, S, H, I = (1, 64, 512, 1536)

        def _quantized_matmul(x, w, scale):
            wq = w.astype(jnp.float8_e4m3fn).astype(x.dtype)
            y = jnp.einsum('bsi,io->bso', x, wq)
            return y * scale
        key = jax.random.key(seed)
        ks = jax.random.split(key, 7)
        return {'x': jax.random.normal(ks[0], (B, S, H), dtype=jnp.float32), 'gate_w': jax.random.normal(ks[1], (H, I), dtype=jnp.float32) * 0.02, 'up_w': jax.random.normal(ks[2], (H, I), dtype=jnp.float32) * 0.02, 'down_w': jax.random.normal(ks[3], (I, H), dtype=jnp.float32) * 0.02, 'gate_scale': jax.random.uniform(ks[4], (I,), dtype=jnp.float32, minval=0.5, maxval=1.5), 'up_scale': jax.random.uniform(ks[5], (I,), dtype=jnp.float32, minval=0.5, maxval=1.5), 'down_scale': jax.random.uniform(ks[6], (H,), dtype=jnp.float32, minval=0.5, maxval=1.5)}
    _L0_ffn_in = _L0_ffn_setup()
    _d = {'L0_attn_x': _L0_attn_in['x'], 'L0_attn_Wq': _L0_attn_in['Wq'], 'L0_attn_Wk': _L0_attn_in['Wk'], 'L0_attn_Wv': _L0_attn_in['Wv'], 'L0_attn_Wo': _L0_attn_in['Wo'], 'L0_attn_bo': _L0_attn_in['bo'], 'L0_ffn_gate_w': _L0_ffn_in['gate_w'], 'L0_ffn_up_w': _L0_ffn_in['up_w'], 'L0_ffn_down_w': _L0_ffn_in['down_w'], 'L0_ffn_gate_scale': _L0_ffn_in['gate_scale'], 'L0_ffn_up_scale': _L0_ffn_in['up_scale'], 'L0_ffn_down_scale': _L0_ffn_in['down_scale']}
    _x0 = _d['L0_attn_x']
    _d['L0_attn_x'] = jax.random.normal(jax.random.fold_in(jax.random.key(seed), 1), (4, 1024, 512), dtype=_x0.dtype)
    del _x0
    return _d

def reference(L0_attn_x, L0_attn_Wq, L0_attn_Wk, L0_attn_Wv, L0_attn_Wo, L0_attn_bo, L0_ffn_gate_w, L0_ffn_up_w, L0_ffn_down_w, L0_ffn_gate_scale, L0_ffn_up_scale, L0_ffn_down_scale):

    def _L0_attn_ref(x, Wq, Wk, Wv, Wo, bo):
        import jax, jax.numpy as jnp
        import numpy as np
        WIDTH = 512
        NUM_HEADS = 16
        HEAD_DIM = WIDTH // NUM_HEADS
        ROPE_DIMS = HEAD_DIM // 2
        WINDOW = 128
        ROPE_BASE = 10000.0
        NEG_INF = -1000000000.0

        def apply_rope(x, dims, offset=0, base=ROPE_BASE):
            L = x.shape[2]
            half = dims // 2
            pos = (offset + jnp.arange(L)).astype(x.dtype)
            inv_freq = jnp.exp(-jnp.log(jnp.asarray(base, x.dtype)) * (jnp.arange(0, dims, 2).astype(x.dtype) / dims))
            theta = pos[:, None] * inv_freq[None, :]
            cos = jnp.cos(theta)[None, None]
            sin = jnp.sin(theta)[None, None]
            x1 = x[..., :half]
            x2 = x[..., half:dims]
            rest = x[..., dims:]
            rx1 = x1 * cos - x2 * sin
            rx2 = x1 * sin + x2 * cos
            return jnp.concatenate([rx1, rx2, rest], axis=-1)
        B, L, D = x.shape
        H, hd = (NUM_HEADS, HEAD_DIM)
        scale = hd ** (-0.5)
        q = (x @ Wq).reshape(B, L, H, hd).transpose(0, 2, 1, 3)
        k = (x @ Wk).reshape(B, L, 1, hd).transpose(0, 2, 1, 3)
        v = (x @ Wv).reshape(B, L, 1, hd).transpose(0, 2, 1, 3)
        q = apply_rope(q, ROPE_DIMS)
        k = apply_rope(k, ROPE_DIMS)
        i = jnp.arange(L)[:, None]
        j = jnp.arange(L)[None, :]
        allowed = (i - j >= 0) & (i - j < WINDOW)
        mask = jnp.where(allowed, 0.0, NEG_INF).astype(x.dtype)
        scores = jnp.einsum('bhqd,bkd->bhqk', q, k[:, 0]) * scale
        scores = scores + mask[None, None]
        attn = jax.nn.softmax(scores, axis=-1)
        out = jnp.einsum('bhqk,bkd->bhqd', attn, v[:, 0])
        out = out.transpose(0, 2, 1, 3).reshape(B, L, D)
        return out @ Wo + bo

    def _L0_ffn_ref(x, gate_w, up_w, down_w, gate_scale, up_scale, down_scale):
        import jax, jax.numpy as jnp
        import numpy as np
        B, S, H, I = (1, 64, 512, 1536)

        def _quantized_matmul(x, w, scale):
            wq = w.astype(jnp.float8_e4m3fn).astype(x.dtype)
            y = jnp.einsum('bsi,io->bso', x, wq)
            return y * scale
        gate = jax.nn.silu(_quantized_matmul(x, gate_w, gate_scale))
        up = _quantized_matmul(x, up_w, up_scale)
        fuse = gate * up
        return _quantized_matmul(fuse, down_w, down_scale)
    x = L0_attn_x
    x = _layernorm(x + _L0_attn_ref(x, L0_attn_Wq, L0_attn_Wk, L0_attn_Wv, L0_attn_Wo, L0_attn_bo), axis=-1)
    x = _layernorm(x + _L0_ffn_ref(x, L0_ffn_gate_w, L0_ffn_up_w, L0_ffn_down_w, L0_ffn_gate_scale, L0_ffn_up_scale, L0_ffn_down_scale), axis=-1)
    return x

_drawn_inputs = setup_inputs


def setup_inputs(seed=0):
    import zlib

    import numpy as np

    out = dict(_drawn_inputs(seed))
    spreads = {}
    factors = {'L0_attn_Wq': 8.0, 'L0_attn_Wk': 8.0, 'L0_attn_bo': 2.746}
    for name, (base, spread) in spreads.items():
        noise = np.random.default_rng([zlib.crc32(name.encode()), seed]).standard_normal(out[name].shape)
        drawn = base * np.exp(spread * noise) if base else spread * noise
        out[name] = jnp.asarray(drawn.astype(out[name].dtype))
    for name, factor in factors.items():
        out[name] = (out[name] * factor).astype(out[name].dtype)
    return out
```

```python
from contextlib import ExitStack

import numpy as np

import concourse.bass as bass
from concourse import mybir

F32 = mybir.dt.float32
F32R = mybir.dt.float32r
I32 = mybir.dt.int32
U8 = mybir.dt.uint8
ALU = mybir.AluOpType
ACT = mybir.ActivationFunctionType
AX_X = mybir.AxisListType.X

P = 128
D = 512
H = 16
HD = 32
ROPE = HD // 2
DC = D // P
I = 1536
IC = I // P
TILES = 2
T = TILES * P
HQ = 4
NQ = H // HQ
SCALE = HD ** -0.5
EPS = 1e-5
NEG = -1e30
ROW = HD + ROPE + 1
PAD = 3 * HD

EXP_BITS = 0x7F800000
ROUND = 1.5 * 2.0 ** 20
ROUND_MIN = ROUND * 2.0 ** -6
OVER = float(np.float32(np.finfo(np.float32).max / 464))
OVER_BACK = float(np.float32(1.0 / np.float64(OVER)))
CHUNKS = 3 * IC
HID = 3
RING = 3


ORDER = {
    "tensor": """
        QT.0.1:1 X1T:2 QT.0.2:1 QT.0.3:1 S.0.0:1 G.0:2 U.0:2 G.1:2 S.0.1:1 U.1:2 G.2:2 U.2:2 S.0.2:1 PT.0.0:1
        DN.0:2 G.3:2 U.3:2 S.0.3:1 DN.1:2 G.4:2 U.4:2 PT.0.1:1 Q.1:1 PV.0.0:1 DN.2:2 G.5:2 PT.0.2:1 U.5:2
        PV.0.1:1 PT.0.3:1 QT.1.0:1 QT.1.1:1 DN.3:2 QT.1.2:1 G.6:2 QT.1.3:1 U.6:2 PV.0.2:1 S.1.0:1 DN.4:2 G.7:2
        PV.0.3:1 RT.0:1 S.1.1:1 U.7:2 DN.5:2 G.8:2 U.8:2 S.1.2:1 WO.0:1 DN.6:2 S.1.3:1 G.9:2 PT.1.0:1 U.9:2
        DN.7:2 XT:0 PT.1.1:1 PV.1.0:1 G.10:2 U.10:2 PT.1.2:1 PV.1.1:1 KV:0 PT.1.3:1 DN.8:2 PV.1.2:1 G.11:2 U.11:2
        PV.1.3:1 RT.1:1 KT:0 Q.0:0 DN.9:2 WO.1:1 DN.10:2 DN.11:2 QT.0.0:0
    """,
    "vector": """
        A1.0:3 A2.0:3 W.22:2 S.0.1:2 A1.1:3 W.0:0 W.23:2 A2.1:3 A1.2:3 S.0.2:2 SUM.0.0:2 W.13:1 W.24:2 A2.2:3
        PT.0.0:2 S.0.3:2 A1.3:3 PM.0.0:2 A2.3:3 SUM.0.1:2 PT.0.1:2 W.25:2 Q.1:2 A1.4:3 W.1:0 PM.0.1:2 W.26:2
        SUM.0.2:2 PT.0.2:2 A2.4:3 PM.0.2:2 A1.5:3 A2.5:3 SUM.0.3:2 W.27:2 W.2:0 PT.0.3:2 R.0:2 W.28:2 A1.6:3
        PM.0.3:2 A2.6:3 S.1.0:2 W.29:2 W.3:0 O1.0:2 S.1.1:2 O3.0:2 A1.7:3 W.14:1 W.4:0 W.30:2 A2.7:3 A1.8:3
        S.1.2:2 A2.8:3 LN1.0:2 W.15:1 W.16:1 SUM.1.0:2 W.31:2 S.1.3:2 W.5:0 W.6:0 PT.1.0:2 W.7:0 PM.1.0:2 A1.9:3
        SUM.1.1:2 PT.1.1:2 PM.1.1:2 W.8:0 XT:1 W.32:2 SUM.1.2:2 PT.1.2:2 PM.1.2:2 W.33:2 A2.9:3 W.17:1 A1.10:3
        PT.1.3:2 SUM.1.3:2 W.9:0 PM.1.3:2 KV:1 R.1:2 A2.10:3 KH:1 W.18:1 O1.1:2 A1.11:3 A2.11:3 W.34:2 O3.1:2
        W.10:0 Q.0:1 W.11:0 W.19:1 W.20:1 LN2.0:2 W.12:0 LN1.1:2 W.21:1 W.35:2 Y:3 LN2.1:2 W.36:2 YA:3 W.37:2
        X1T:2 YN:3 S.0.0:1
    """,
    "scalar": """
        W.0:0 W.22:2 A1.1:3 B.0:3 W.12:1 E.0.0:2 W.13:1 A1.2:3 S.0.2:2 PT.0.0:2 W.23:2 B.1:3 A1.3:3 S.0.3:2 B.2:3
        E.0.1:2 PT.0.1:2 E.0.2:2 W.24:2 W.1:0 A1.4:3 W.2:0 W.14:1 W.25:2 W.3:0 B.3:3 W.4:0 QH.1:2 W.26:2 PT.0.2:2
        E.0.3:2 W.5:0 A1.5:3 QT.1.0:2 QT.1.1:2 W.6:0 QT.1.2:2 PT.0.3:2 QT.1.3:2 W.27:2 B.4:3 A1.6:3 W.7:0 W.28:2
        S.1.0:2 B.5:3 RT.0:2 S.1.1:2 A1.7:3 O2.0:2 W.29:2 B.6:3 A1.8:3 S.1.2:2 W.15:1 B.7:3 E.1.0:2 S.1.3:2
        W.30:2 PT.1.0:2 W.31:2 W.8:0 W.9:0 E.1.1:2 A1.9:3 PT.1.1:2 XT:1 E.1.2:2 B.8:3 W.16:1 PT.1.2:2 E.1.3:2
        W.32:2 A1.10:3 PT.1.3:2 B.9:3 KV:1 KH:1 W.17:1 W.18:1 W.33:2 A1.11:3 RT.1:2 O2.1:2 B.10:3 W.34:2 KT:1
        W.10:0 W.11:0 B.11:3 QH.0:1 W.19:1 W.35:2 QT.0.0:1 QT.0.1:1 W.20:1 X1T:2 QT.0.2:1 QT.0.3:1 S.0.0:1 W.21:1
        A1.0:2 S.0.1:1
    """,
    "gpsimd": """
        W.20:2 W.35:3 W.21:2 W.36:3 W.11:1 S.0.0:2 B.0:3 W.1:0 W.22:2 S.0.1:2 W.12:1 B.1:3 W.23:2 S.0.2:2 W.13:1
        XB:2 PM.0.0:2 W.2:0 W.24:2 B.2:3 S.0.3:2 W.25:2 PM.0.1:2 B.3:3 QH.1:2 W.26:2 W.3:0 PM.0.2:2 W.14:1 W.27:2
        B.4:3 W.4:0 PM.0.3:2 W.15:1 W.28:2 W.16:1 W.29:2 B.5:3 W.17:1 W.5:0 S.1.0:2 B.6:3 W.30:2 S.1.1:2 B.7:3
        LN1.0:2 W.6:0 PM.1.0:2 W.31:2 W.7:0 S.1.2:2 S.1.3:2 W.18:1 W.8:0 PM.1.1:2 W.9:0 B.8:3 W.32:2 PM.1.2:2
        B.9:3 PM.1.3:2 B.10:3 KV:1 W.33:2 W.34:2 B.11:3 QH.0:1 W.19:1 W.10:0 LN1.1:2 Y:3
    """,
    "sync": """
        C.10:1 C.29:3 C.11:1 C.0:0 C.1:0 C.18:2 C.30:3 C.19:2 C.20:2 C.21:2 C.22:2 C.31:3 C.23:2 C.32:3 C.2:0
        C.3:0 C.24:2 C.4:0 C.5:0 C.12:1 C.25:2 C.6:0 C.26:2 C.13:1 C.14:1 C.27:2 C.33:3 C.34:3 C.35:3 C.28:2
        C.7:0 LD:1 C.15:1 C.16:1 C.17:1 ST:3 C.8:0 C.9:0
    """,
}


def order_of(engine):
    steps = []
    for word in ORDER[engine].split():
        name, age = word.split(":")
        name, *at = name.split(".")
        steps.append((int(age), (name, *map(int, at))))
    return steps


ONCE = ("C", "W")
AGES = 1 + max(age for engine in ORDER for age, _ in order_of(engine))


def layer_kernel(nc, x, wq, wk, wv, wo, bo, gate_w, up_w, down_w, gate_s, up_s, down_s, rows, ident_d, seen_d, out):
    TOKENS = x.shape[0]
    GROUPS = TOKENS // T
    BEFORE = AGES + 1
    PAIRS = (GROUPS - BEFORE) // 2
    assert TOKENS % T == 0 and PAIRS > 0 and x.shape[1] == D

    with ExitStack() as ctx:
        def sb(name, shape, dt=F32):
            return ctx.enter_context(nc.sbuf_tensor(name, shape, dt))

        pair = ctx.enter_context(nc.psum_tensor("pair", [P, 2, 512], F32))
        turned = ctx.enter_context(nc.psum_tensor("turned", [P, 2, 512], F32))
        bank_a, bank_b, bank_c, bank_d = pair[:, 0, :], pair[:, 1, :], turned[:, 0, :], turned[:, 1, :]
        gu = ctx.enter_context(nc.psum_tensor("gu", [P, 2, 2, T], F32))
        down = ctx.enter_context(nc.psum_tensor("down", [P, TILES, D], F32))

        wq_hi, wq_lo = sb("wq_hi", [P, DC, D], F32R), sb("wq_lo", [P, DC, D], F32R)
        wkv_hi, wkv_lo = sb("wkv_hi", [P, DC, 2 * HD], F32R), sb("wkv_lo", [P, DC, 2 * HD], F32R)
        wo_hi, wo_lo = sb("wo_hi", [P, HQ, D], F32R), sb("wo_lo", [P, HQ, D], F32R)
        gate_q, up_q = sb("gate_q", [P, IC, DC, P], F32R), sb("up_q", [P, IC, DC, P], F32R)
        down_q = sb("down_q", [P, IC, D], F32R)
        ident = sb("ident", [P, P])
        seen_k = sb("seen_k", [P, P])
        seen_q = sb("seen_q", [P, P], U8)
        bias_o = sb("bias_o", [P, D])
        scale_d = sb("scale_d", [P, D])
        scale_gu = sb("scale_gu", [P, 2 * IC])
        half_g = sb("half_g", [P, IC])
        half_gu = sb("half_gu", [P, IC])
        minus_half = sb("minus_half", [P, 1])
        eps = sb("eps", [P, 1])
        round_min = sb("round_min", [P, 1])
        stage = sb("stage", [P, RING, 2, 512])
        mlp_tmp = stage[:].rearrange("p r s n -> p (r s n)")
        tanh_t = mlp_tmp[:, 0:2 * T].rearrange("p (b n) -> p b n", b=2)
        silu_t = mlp_tmp[:, 2 * T:4 * T].rearrange("p (b n) -> p b n", b=2)
        hid_t = mlp_tmp[:, 4 * T:6 * T].rearrange("p (b n) -> p b n", b=2)
        down_t = mlp_tmp[:, 6 * T:6 * T + TILES * D].rearrange("p (a n) -> p a n", a=TILES)
        xin = sb("xin", [P, TILES, D])
        pos = sb("pos", [P, 2, TILES, ROW])
        x1 = sb("x1", [P, 2, TILES, D])
        mask_in = x1[:, 1, 0, 0:P]
        scale_in = x1[0:2 * IC, 1, 1, 0:P]
        xt_hi, xt_lo = sb("xt_hi", [P, DC, T], F32R), sb("xt_lo", [P, DC, T], F32R)
        x1t_hi, x1t_lo = sb("x1t_hi", [P, DC, T], F32R), sb("x1t_lo", [P, DC, T], F32R)
        q_part = sb("q_part", [P, H, 4, HD])
        q_rot = q_part[:, :, 3, :]
        q_tmp = q_part[:, :, 1, 0:ROPE]
        q_part_hi = q_part[:].rearrange("p h (u v) n -> p h u v n", v=2)[:, :, :, 0, :]
        q_part_lo = q_part[:].rearrange("p h (u v) n -> p h u v n", v=2)[:, :, :, 1, :]
        q_stack = sb("q_stack", [P, H, P], F32R)
        k_part = sb("k_part", [P, TILES, 4, HD])
        k_rot = k_part[:, :, 3, :]
        k_tmp = k_part[:, :, 1, 0:ROPE]
        k_stack = sb("k_stack", [P, 4, P], F32R)
        v_f = sb("v_f", [P, 4, HD])
        vd = sb("vd", [P, TILES, HD])
        padded = sb("padded", [P, PAD + 16 * P], F32R)
        values = padded[:, PAD:].rearrange("p (s n) -> p s n", n=P)[:, :, 0:HD]
        v_hi, v_lo, vd_hi, vd_lo = values[:, 0:4, :], values[:, 4:8, :], values[:, 8:12, :], values[:, 12:16, :]
        prob_of = [sb(f"prob{a}", [P, H, P]) for a in range(TILES)]
        top = sb("top", [P, H])
        total_of = [sb(f"total{a}", [P, H]) for a in range(TILES)]
        recip = sb("recip", [P, H])
        recip_w = sb("recip_w", [P, HQ, NQ, HD])
        pt_hi, pt_lo = sb("pt_hi", [P, 2, HQ, P], F32R), sb("pt_lo", [P, 2, HQ, P], F32R)
        ptc_hi, ptc_lo = sb("ptc_hi", [P, HQ, P], F32R), sb("ptc_lo", [P, HQ, P], F32R)
        recip_t = sb("recip_t", [P, HQ * P])
        o_f = recip_t
        o_hi, o_lo = sb("o_hi", [P, HQ * P], F32R), sb("o_lo", [P, HQ * P], F32R)
        hid_hi, hid_lo = sb("hid_hi", [P, HID, T], F32R), sb("hid_lo", [P, HID, T], F32R)
        stats, mean_var, rstd = sb("stats", [P, TILES, 6]), sb("mean_var", [P, TILES, 2]), sb("rstd", [P, TILES])
        stats2, mean_var2, rstd2 = sb("stats2", [P, TILES, 6]), sb("mean_var2", [P, TILES, 2]), sb("rstd2", [P, TILES])

        def signal(name, per=1):
            return ctx.enter_context(nc.semaphore(name)), per

        def wait(eng, sig, g, k):
            sem, per = sig
            reg, off = g
            at = off * per + k
            if reg is not None:
                assert at > 0
                eng.wait_ge(sem, reg * (2 * per) + at)
            elif at > 0:
                eng.wait_ge(sem, at)

        passed = ctx.enter_context(nc.semaphore("passed"))

        def hold(eng):
            eng.sem_inc(passed, 1)

        x_in = signal("x_in", 32)
        w_in = [signal(f"w_in_{n}") for n in ("k", "v", "q", "o")]
        c_in = signal("c_in")
        chunk_in = [signal(f"chunk_in{s}") for s in range(RING)]
        y_out = signal("y_out", 16)
        zeroed = signal("zeroed")
        w_hi = signal("w_hi")
        w_lo = signal("w_lo")
        seen_done = signal("seen_done")
        scales_t = signal("scales_t")
        scales_c = signal("scales_c")
        expo_done = signal("expo_done")
        magic_a, magic_done = signal("magic_a"), signal("magic_done")
        added = signal("added")
        taken = signal("taken")
        quantised = signal("quantised")
        xt_full = signal("xt_full")
        kv_full = signal("kv_full")
        q_full = signal("q_full", 2)
        kt_full = signal("kt_full")
        qt_full = signal("qt_full", 8)
        s_full = signal("s_full", 8)
        pt_full = signal("pt_full", 8)
        pv_done = signal("pv_done", 8)
        rt_full = signal("rt_full", 2)
        wo_full = signal("wo_full", 2)
        x1t_full = signal("x1t_full")
        xt_hi_done = signal("xt_hi_done")
        xt_split = signal("xt_split")
        xb_done = signal("xb_done")
        v_hi_done = signal("v_hi_done")
        k_hi_done = signal("k_hi_done")
        k_rotated = signal("k_rotated")
        kv_read = signal("kv_read")
        k_split = signal("k_split")
        vd_split = signal("vd_split")
        kt_copied = signal("kt_copied")
        q_rotated = signal("q_rotated", 2)
        q_hi_done = signal("q_hi_done", 2)
        q_split = signal("q_split", 2)
        qt_copied = signal("qt_copied", 8)
        prev_copied = signal("prev_copied", 8)
        s_merged = signal("s_merged", 8)
        max_done = signal("max_done", 8)
        sub_done = signal("sub_done", 8)
        exp_done = signal("exp_done", 8)
        sum_done = signal("sum_done", 8)
        recip_done = signal("recip_done", 2)
        pt_hi_done = signal("pt_hi_done", 8)
        pt_split = signal("pt_split", 8)
        pt_masked = signal("pt_masked", 8)
        rt_copied = signal("rt_copied", 2)
        o_scaled = signal("o_scaled", 2)
        o_hi_done = signal("o_hi_done", 2)
        o_split = signal("o_split", 2)
        wo_added = signal("wo_added", 2)
        var_done = signal("var_done", 2)
        rstd_done = signal("rstd_done", 2)
        x1_done = signal("x1_done", 2)
        x1t_hi_done = signal("x1t_hi_done")
        x1t_split = signal("x1t_split")
        gu_full = signal("gu_full", IC)
        tanh_done = signal("tanh_done", IC)
        silu_done = signal("silu_done", IC)
        hid_done = signal("hid_done", IC)
        hid_hi_done = signal("hid_hi_done", IC)
        hid_split = signal("hid_split", IC)
        down_done = signal("down_done", IC)
        down_read = signal("down_read", 2)
        y_added = signal("y_added", 2)
        var2_done = signal("var2_done", 2)
        rstd2_done = signal("rstd2_done", 2)
        y_done = signal("y_done", 2)
        kv_own = signal("kv_own", 3)
        q_own = signal("q_own", 4)
        recip_own = signal("recip_own", 2)
        stats_own = signal("stats_own", 2)
        stats2_own = signal("stats2_own", 2)
        vd_own = signal("vd_own", 2)
        root_own = signal("root_own", 2)
        root2_own = signal("root2_own", 2)
        ptc_lo_done = signal("ptc_lo_done", 8)

        block = ctx.enter_context(nc.Block())

        def run(eng, order, step):
            def peeled(n):
                for age, s in order:
                    if 0 <= n - age < (1 if s[0] in ONCE else GROUPS):
                        step(s, (None, n - age))

            for n in range(BEFORE):
                peeled(n)
            with eng.Fori(0, PAIRS) as j:
                for n in (BEFORE, BEFORE + 1):
                    for age, s in order:
                        if s[0] not in ONCE:
                            step(s, (j, n - age))
            for n in range(BEFORE + 2 * PAIRS, GROUPS + AGES - 1):
                peeled(n)

        def chunk_src(k):
            i, kind = divmod(k, 3)
            if kind == 2:
                return down_w[i * P:(i + 1) * P, :]
            w = (gate_w, up_w)[kind]
            return w.rearrange("(c p) n -> p c n", p=P)[:, :, i * P:(i + 1) * P]

        def chunk_dst(k):
            i, kind = divmod(k, 3)
            return down_q[:, i, :] if kind == 2 else (gate_q, up_q)[kind][:, i, :, :].rearrange("p c n -> p (c n)")

        wk_stage = stage[:, 2, 0, 0:DC * HD].rearrange("p (c n) -> p c n", c=DC)
        wv_stage = stage[:, 2, 1, 0:DC * HD].rearrange("p (c n) -> p c n", c=DC)
        wq_stage = prob_of[0][:].rearrange("p h n -> p (h n)").rearrange("p (c n) -> p c n", c=DC)
        wo_stage = stage[:, 0:2, :, :].rearrange("p r s n -> p (r s) n")
        attention_weights = [(wkv_hi[:, :, 0:HD], wkv_lo[:, :, 0:HD], wk_stage), (wkv_hi[:, :, HD:], wkv_lo[:, :, HD:], wv_stage),
                             (wq_hi[:], wq_lo[:], wq_stage), (wo_hi[:], wo_lo[:], wo_stage)]

        @block.sync
        def _(sp):
            x_t = x.rearrange("(t p) d -> p t d", p=P)
            rows_t = rows.rearrange("(t p) d -> p t d", p=P)
            out_t = out.rearrange("(t p) d -> p t d", p=P)

            def load_x(g):
                reg, off = g
                wait(sp, xt_full, g, 0)
                hold(sp)
                wait(sp, xb_done, g, 0)
                hold(sp)
                wait(sp, q_rotated, (reg, off - 1), 0)
                hold(sp)
                wait(sp, prev_copied, (reg, off - 1), 0)
                hold(sp)
                first = off * TILES if reg is None else reg * (2 * TILES) + off * TILES
                ts = bass.ds(first, TILES)
                sp.dma_start(xin[:], x_t[:, ts, :]).then_inc(x_in[0], 16)
                sp.dma_start(pos[:, off % 2, :, :], rows_t[:, ts, :]).then_inc(x_in[0], 16)

            def step(s, g):
                if s[0] == "ST":
                    store_y(g)
                elif s[0] == "C":
                    load_chunk(s[1])
                elif g[0] is not None or g[1] > 0:
                    load_x(g)

            sp.dma_start(ident[:], ident_d).then_inc(c_in[0], 16)
            load_x((None, 0))
            for n, (dst, src) in enumerate(((wk_stage, wk), (wv_stage, wv), (wq_stage, wq))):
                sp.dma_start(dst, src.rearrange("(c p) n -> p c n", p=P)).then_inc(w_in[n][0], 16)
            for r in range(NQ):
                sp.dma_start(wo_stage[r * HD:(r + 1) * HD, :, :],
                             wo[r * P:(r + 1) * P, :].rearrange("(c d) n -> d c n", d=HD)).then_inc(w_in[3][0], 16)
            sp.dma_start(seen_k[:], seen_d[0]).then_inc(c_in[0], 16)
            sp.dma_start(mask_in, seen_d[1]).then_inc(c_in[0], 16)
            sp.dma_start(bias_o[:], bo.partition_broadcast(P)).then_inc(c_in[0], 16)
            sp.dma_start(scale_d[:], down_s.partition_broadcast(P)).then_inc(c_in[0], 16)
            sp.dma_start(scale_in[0:IC], gate_s.rearrange("(i p) -> i p", p=P)).then_inc(c_in[0], 16)
            sp.dma_start(scale_in[IC:2 * IC], up_s.rearrange("(i p) -> i p", p=P)).then_inc(c_in[0], 16)
            sp.wait_ge(w_lo[0], 4)

            def load_chunk(k):
                if k >= RING:
                    sp.wait_ge(quantised[0], k - RING + 1)
                dst = stage[:, k % RING, 0, :]
                sp.dma_start(dst if k % 3 == 2 else dst.rearrange("p (c n) -> p c n", c=DC),
                             chunk_src(k)).then_inc(chunk_in[k % RING][0], 16)

            def store_y(g):
                reg, off = g
                wait(sp, y_done, g, 2)
                hold(sp)
                first = off * TILES if reg is None else reg * (2 * TILES) + off * TILES
                sp.dma_start(out_t[:, bass.ds(first, TILES), :], x1[:, off % 2, :, :]).then_inc(y_out[0], 16)

            run(sp, order_of("sync"), step)
            sp.wait_ge(y_out[0], 16 * GROUPS)

        @block.tensor
        def _(pe):
            def split_product(bank, lhs_hi, lhs_lo, rhs_hi, rhs_lo, n):
                for c in range(n):
                    nc.tensor.matmul(bank, lhs_hi(c), rhs_hi(c), start=(c == 0), stop=False)
                    nc.tensor.matmul(bank, lhs_hi(c), rhs_lo(c), start=False, stop=False)
                    last = nc.tensor.matmul(bank, lhs_lo(c), rhs_hi(c), start=False, stop=(c == n - 1))
                return last

            def step(s, g):
                what, args = s[0], s[1:]
                reg, off = g
                par = off % 2
                if what == "XT":
                    if off == 0 and reg is None:
                        pe.wait_ge(c_in[0], 16)
                    wait(pe, x_in, g, 32)
                    wait(pe, s_merged, g, 0)
                    for c in range(DC):
                        for a in range(TILES):
                            col = (c % 2) * T + a * P
                            last = nc.tensor.transpose(pair[:, c // 2, col:col + P],
                                                       xin[:, a, c * P:(c + 1) * P], ident[:])
                    last.then_inc(xt_full[0], 1)
                elif what == "KV":
                    if off == 0 and reg is None:
                        pe.wait_ge(w_lo[0], 2)
                        pe.wait_ge(w_hi[0], 2)
                    wait(pe, xt_split, g, 1)
                    for a in range(TILES):
                        last = split_product(bank_a[:, a * 2 * HD:(a + 1) * 2 * HD],
                                             lambda c: xt_hi[:, c, a * P:(a + 1) * P],
                                             lambda c: xt_lo[:, c, a * P:(a + 1) * P],
                                             lambda c: wkv_hi[:, c, :], lambda c: wkv_lo[:, c, :], DC)
                    last.then_inc(kv_full[0], 1)
                elif what == "Q":
                    a, = args
                    if off == 0 and reg is None and a == 0:
                        pe.wait_ge(w_lo[0], 3)
                    if a == 0:
                        wait(pe, kv_read, g, 1)
                        wait(pe, k_split, g, 1)
                    else:
                        wait(pe, s_merged, g, 4)
                    split_product(bank_a, lambda c: xt_hi[:, c, a * P:(a + 1) * P],
                                  lambda c: xt_lo[:, c, a * P:(a + 1) * P],
                                  lambda c: wq_hi[:, c, :], lambda c: wq_lo[:, c, :], DC).then_inc(q_full[0], 1)
                elif what == "KT":
                    wait(pe, k_split, g, 1)
                    for a in range(TILES):
                        last = nc.tensor.transpose(bank_b[:, a * P:(a + 1) * P],
                                                   k_part[:, a, :, :].rearrange("p u n -> p (u n)"), ident[:])
                    last.then_inc(kt_full[0], 1)
                elif what == "QT":
                    a, r = args
                    wait(pe, q_split, g, a + 1)
                    if r == 0 and a == 0:
                        wait(pe, kt_copied, g, 1)
                    elif r >= 2:
                        wait(pe, qt_copied, g, 4 * a + r - 1)
                    bank = bank_a if r % 2 else bank_b
                    for n in range(HQ):
                        last = nc.tensor.transpose(bank[:, n * P:(n + 1) * P],
                                                   q_part[:, HQ * r + n, :, :].rearrange("p u n -> p (u n)"), ident[:])
                    last.then_inc(qt_full[0], 1)
                elif what == "S":
                    a, r = args
                    if r == 0:
                        wait(pe, qt_copied, g, 4 * a + 4)
                    else:
                        wait(pe, s_merged, g, 4 * a + r)
                    slot = 2 * par + a
                    keys = k_stack[:, slot - 1:slot + 1, :] if slot else k_stack[:, 3::-3, :]
                    for n in range(HQ):
                        last = nc.tensor.matmul(pair[:, n // 2, (n % 2) * 2 * P:(n % 2 + 1) * 2 * P],
                                                q_stack[:, HQ * r + n, :], keys, start=True, stop=True)
                    last.then_inc(s_full[0], 1)
                elif what == "PT":
                    a, r = args
                    wait(pe, exp_done, g, 4 * a + r + 1)
                    if r > 0:
                        wait(pe, pt_split, g, 4 * a + r)
                    elif a == 0:
                        wait(pe, x1t_split, g, 0)
                    else:
                        wait(pe, wo_added, g, 1)
                    for n in range(HQ):
                        last = nc.tensor.transpose(bank_c[:, n * P:(n + 1) * P],
                                                   prob_of[a][:, HQ * r + n, :], ident[:])
                    last.then_inc(pt_full[0], 1)
                elif what == "PV":
                    a, r = args
                    wait(pe, pt_split, g, 4 * a + r + 1)
                    wait(pe, pt_masked, g, 4 * a + r + 1)
                    wait(pe, ptc_lo_done, g, 4 * a + r + 1)
                    if r == 0 and a == 0:
                        wait(pe, vd_split, g, 1)
                    elif r == 0:
                        wait(pe, o_scaled, g, 1)
                    prev = (2 * par + a - 1) % 4

                    def window(slot):
                        return padded[:, slot * P + PAD - HD * r:slot * P + PAD - HD * r + P]

                    hi, lo = pt_hi[:, r % 2, :, :], pt_lo[:, r % 2, :, :]
                    here = 2 * par + a
                    pairs = [(window(prev), hi), (window(4 + prev), hi), (window(prev), lo), (window(8 + here), ptc_hi[:]),
                             (window(12 + here), ptc_hi[:]), (window(8 + here), ptc_lo[:])]
                    for n, (v, p) in enumerate(pairs):
                        last = nc.tensor.matmul(bank_d, v, p, start=(r == 0 and n == 0), stop=(r == NQ - 1 and n == 5))
                    last.then_inc(pv_done[0], 1)
                elif what == "RT":
                    a, = args
                    wait(pe, recip_done, g, a + 1)
                    for c in range(HQ):
                        last = nc.tensor.transpose(bank_c[:, c * P:(c + 1) * P],
                                                   recip_w[:, c, :, :].rearrange("p r n -> p (r n)"), ident[:])
                    last.then_inc(rt_full[0], 1)
                elif what == "WO":
                    a, = args
                    if off == 0 and reg is None and a == 0:
                        pe.wait_ge(w_lo[0], 4)
                    wait(pe, o_split, g, a + 1)
                    split_product(bank_c, lambda c: o_hi[:, c * P:(c + 1) * P], lambda c: o_lo[:, c * P:(c + 1) * P],
                                  lambda c: wo_hi[:, c, :], lambda c: wo_lo[:, c, :], HQ).then_inc(wo_full[0], 1)
                elif what == "X1T":
                    wait(pe, x1_done, g, 2)
                    for c in range(DC):
                        for a in range(TILES):
                            col = (c % 2) * T + a * P
                            last = nc.tensor.transpose(turned[:, c // 2, col:col + P],
                                                       x1[:, par, a, c * P:(c + 1) * P], ident[:])
                    last.then_inc(x1t_full[0], 1)
                elif what in ("G", "U"):
                    i, = args
                    u = int(what == "U")
                    if off == 0 and reg is None and i == 0 and u == 0:
                        pe.wait_ge(quantised[0], CHUNKS)
                    if i == 0 and u == 0:
                        wait(pe, x1t_split, g, 1)
                    if u == 0:
                        wait(pe, hid_done, g, i - 1)
                    w = (gate_q, up_q)[u]
                    for c in range(DC):
                        nc.tensor.matmul(gu[:, i % 2, u, :], w[:, i, c, :], x1t_hi[:, c, :], start=(c == 0), stop=False)
                        last = nc.tensor.matmul(gu[:, i % 2, u, :], w[:, i, c, :], x1t_lo[:, c, :], start=False,
                                                stop=(c == DC - 1))
                    if u:
                        last.then_inc(gu_full[0], 1)
                elif what == "DN":
                    i, = args
                    wait(pe, hid_split, g, i + 1)
                    if i == 0:
                        wait(pe, down_read, g, 0)
                    for a in range(TILES):
                        for n, part in enumerate((hid_hi, hid_lo)):
                            last = nc.tensor.matmul(down[:, a, :], part[:, i % HID, a * P:(a + 1) * P], down_q[:, i, :],
                                                    start=(i == 0 and n == 0), stop=(i == IC - 1 and n == 1))
                    last.then_inc(down_done[0], 1)

            pe.wait_ge(c_in[0], 16 * 7)
            nc.tensor.transpose(gu[:, 0, 0, 0:2 * IC], scale_in, ident[0:2 * IC, 0:2 * IC]).then_inc(scales_t[0], 1)
            run(pe, order_of("tensor"), step)

        @block.scalar
        def _(act):
            def step(s, g):
                what, args = s[0], s[1:]
                reg, off = g
                par = off % 2
                if what == "W":
                    k, = args
                    if k < CHUNKS:
                        t = stage[:, k % RING, 1, :]
                        act.wait_ge(expo_done[0], k + 1)
                        nc.scalar.activation(t, t, ACT.Relu, bias=round_min[:], scale=ROUND).then_inc(magic_a[0], 1)
                        act.wait_ge(magic_a[0], k + 1)
                        nc.scalar.activation(t, t, ACT.Copy, bias=ROUND_MIN).then_inc(magic_done[0], 1)
                elif what == "XT":
                    wait(act, xt_full, g, 1)
                    wait(act, q_full, g, 0)
                    nc.scalar.activation(xt_hi[:].rearrange("p c n -> p (c n)"),
                                         pair[:].rearrange("p b n -> p (b n)"), ACT.Copy).then_inc(xt_hi_done[0], 1)
                elif what == "KV":
                    wait(act, kv_full, g, 1)
                    wait(act, pv_done, g, -4)
                    kv = bank_a[:, 0:TILES * 2 * HD].rearrange("p (a n) -> p a n", a=TILES)
                    nc.scalar.activation(v_hi[:, 2 * par:2 * par + 2, :], kv[:, :, HD:2 * HD],
                                         ACT.Copy).then_inc(v_hi_done[0], 1)
                elif what == "KH":
                    wait(act, k_rotated, g, 1)
                    nc.scalar.activation(k_part[:, :, 0:2, :].bitcast(F32R),
                                         k_rot.unsqueeze(2).broadcast_to([P, TILES, 2, HD]), ACT.Copy).then_inc(k_hi_done[0], 1)
                elif what == "QH":
                    a, = args
                    wait(act, q_rotated, g, a + 1)
                    nc.scalar.activation(q_part_hi.bitcast(F32R), q_rot.unsqueeze(2).broadcast_to([P, H, 2, HD]),
                                         ACT.Copy).then_inc(q_hi_done[0], 1)
                elif what == "KT":
                    wait(act, kt_full, g, 1)
                    nc.scalar.activation(k_stack[:, 2 * par:2 * par + 2, :],
                                         bank_b[:, 0:TILES * P].rearrange("p (a n) -> p a n", a=TILES),
                                         ACT.Copy).then_inc(kt_copied[0], 1)
                elif what == "QT":
                    a, r = args
                    wait(act, qt_full, g, 4 * a + r + 1)
                    nc.scalar.activation(q_stack[:, HQ * r:HQ * r + HQ, :],
                                         (bank_a if r % 2 else bank_b).rearrange("p (h n) -> p h n", h=HQ),
                                         ACT.Copy).then_inc(qt_copied[0], 1)
                elif what == "S":
                    a, r = args
                    wait(act, s_full, g, 4 * a + r + 1)
                    wait(act, sum_done, g, 4 * a + r - 7)
                    wait(act, pt_full, g, 4 * a + r - 7)
                    scores = pair[:].rearrange("p b (h s n) -> p (b h) s n", h=2, s=2)
                    nc.scalar.activation(prob_of[a][:, HQ * r:HQ * r + HQ, :], scores[:, :, 0, :], ACT.Identity,
                                         bias=pos[:, par, a, ROW - 1:ROW]).then_inc(prev_copied[0], 1)
                elif what == "E":
                    a, r = args
                    wait(act, sub_done, g, 4 * a + r + 1)
                    q4 = prob_of[a][:, HQ * r:HQ * r + HQ, :].rearrange("p h n -> p (h n)")
                    nc.scalar.activation(q4, q4, ACT.Exp, scale=SCALE).then_inc(exp_done[0], 1)
                elif what == "PT":
                    a, r = args
                    wait(act, pt_full, g, 4 * a + r + 1)
                    wait(act, pv_done, g, 4 * a + r - 1)
                    nc.scalar.activation(pt_hi[:, r % 2, :, :].rearrange("p h n -> p (h n)"), bank_c,
                                         ACT.Copy).then_inc(pt_hi_done[0], 1)
                elif what == "RT":
                    a, = args
                    wait(act, rt_full, g, a + 1)
                    wait(act, o_split, g, a)
                    nc.scalar.activation(recip_t[:], bank_c, ACT.Copy).then_inc(rt_copied[0], 1)
                elif what == "O2":
                    a, = args
                    wait(act, o_scaled, g, a + 1)
                    wait(act, wo_full, g, a)
                    nc.scalar.activation(o_hi[:], o_f[:], ACT.Copy).then_inc(o_hi_done[0], 1)
                elif what == "X1T":
                    wait(act, x1t_full, g, 1)
                    wait(act, gu_full, g, 0)
                    nc.scalar.activation(x1t_hi[:].rearrange("p c n -> p (c n)"),
                                         turned[:].rearrange("p b n -> p (b n)"), ACT.Copy).then_inc(x1t_hi_done[0], 1)
                elif what == "A1":
                    i, = args
                    if off == 0 and reg is None and i == 0:
                        act.wait_ge(scales_c[0], 3)
                    wait(act, gu_full, g, i + 1)
                    wait(act, silu_done, g, i - 1)
                    nc.scalar.activation(tanh_t[:, i % 2, :], gu[:, i % 2, 0, :], ACT.Tanh,
                                         scale=half_g[:, i:i + 1]).then_inc(tanh_done[0], 1)
                elif what == "B":
                    i, = args
                    wait(act, hid_done, g, i + 1)
                    wait(act, down_done, g, i + 1 - HID)
                    nc.scalar.activation(hid_hi[:, i % HID, :], hid_t[:, i % 2, :], ACT.Copy).then_inc(hid_hi_done[0], 1)

            for n, (hi, _, src) in enumerate(attention_weights):
                act.wait_ge(w_in[n][0], 64 if n == 3 else 16)
                nc.scalar.activation(hi, src, ACT.Copy).then_inc(w_hi[0], 1)
            act.wait_ge(zeroed[0], 1)
            run(act, order_of("scalar"), step)

        @block.vector
        def _(dve):
            def step(s, g):
                what, args = s[0], s[1:]
                reg, off = g
                par = off % 2
                if what == "W":
                    k, = args
                    if k < CHUNKS:
                        w, t = stage[:, k % RING, 0, :], stage[:, k % RING, 1, :]
                        dve.wait_ge(chunk_in[k % RING][0], 16 * (k // RING + 1))
                        nc.vector.tensor_scalar(t.bitcast(I32), w.bitcast(I32), EXP_BITS, None,
                                                ALU.bitwise_and).then_inc(expo_done[0], 1)
                    if 1 <= k <= CHUNKS:
                        w, t = stage[:, (k - 1) % RING, 0, :], stage[:, (k - 1) % RING, 1, :]
                        dve.wait_ge(magic_done[0], k)
                        nc.vector.tensor_tensor(w, w, t, ALU.add).then_inc(added[0], 1)
                    if k >= 2:
                        w = stage[:, (k - 2) % RING, 0, :]
                        dve.wait_ge(taken[0], k - 1)
                        nc.vector.tensor_scalar(chunk_dst(k - 2), w, OVER, OVER_BACK, ALU.mult,
                                                ALU.mult).then_inc(quantised[0], 1)
                elif what == "XT":
                    wait(dve, xt_hi_done, g, 1)
                    nc.vector.tensor_tensor(xt_lo[:].rearrange("p c n -> p (c n)"),
                                            pair[:].rearrange("p b n -> p (b n)"),
                                            xt_hi[:].bitcast(F32).rearrange("p c n -> p (c n)"),
                                            ALU.subtract).then_inc(xt_split[0], 1)
                elif what == "KV":
                    wait(dve, x_in, g, 32)
                    wait(dve, v_hi_done, g, 1)
                    kv = bank_a[:, 0:TILES * 2 * HD].rearrange("p (a n) -> p a n", a=TILES)
                    cos, sin = pos[:, par, :, 0:HD], pos[:, par, :, HD:HD + ROPE]
                    nc.vector.tensor_tensor(k_rot, kv[:, :, 0:HD], cos, ALU.mult).then_inc(kv_own[0], 1)
                    swapped = kv[:, :, 0:ROPE].rearrange("p a (u e) -> p a u e", u=2)[:, :, ::-1, :]
                    nc.vector.tensor_tensor(k_tmp.rearrange("p a (u e) -> p a u e", u=2), swapped,
                                            sin.rearrange("p a (u e) -> p a u e", u=2), ALU.mult).then_inc(kv_own[0], 1)
                    nc.vector.tensor_copy(v_f[:, 2 * par:2 * par + 2, :], kv[:, :, HD:2 * HD]).then_inc(kv_own[0], 1)
                    wait(dve, kv_own, g, 2)
                    nc.vector.tensor_tensor(k_rot[:, :, 0:ROPE], k_rot[:, :, 0:ROPE], k_tmp,
                                            ALU.add).then_inc(k_rotated[0], 1)
                    nc.vector.tensor_tensor(v_lo[:, 2 * par:2 * par + 2, :], kv[:, :, HD:2 * HD],
                                            v_hi[:, 2 * par:2 * par + 2, :].bitcast(F32),
                                            ALU.subtract).then_inc(kv_read[0], 1)
                elif what == "KH":
                    wait(dve, k_hi_done, g, 1)
                    nc.vector.tensor_tensor(k_part[:, :, 2:4, :], k_rot.unsqueeze(2).broadcast_to([P, TILES, 2, HD]),
                                            k_part[:, :, 0:2, :], ALU.subtract).then_inc(k_split[0], 1)
                elif what == "Q":
                    a, = args
                    wait(dve, q_full, g, a + 1)
                    wait(dve, q_split, g, a)
                    cos, sin = pos[:, par, a, 0:HD], pos[:, par, a, HD:HD + ROPE]
                    q3 = bank_a.rearrange("p (h n) -> p h n", h=H)
                    nc.vector.tensor_tensor(q_rot, q3, cos.unsqueeze(1).broadcast_to([P, H, HD]),
                                            ALU.mult).then_inc(q_own[0], 1)
                    swapped = q3[:, :, 0:ROPE].rearrange("p h (u e) -> p h u e", u=2)[:, :, ::-1, :]
                    nc.vector.tensor_tensor(q_tmp.rearrange("p h (u e) -> p h u e", u=2), swapped,
                                            sin.rearrange("p (u e) -> p u e", u=2).unsqueeze(1)
                                            .broadcast_to([P, H, 2, ROPE // 2]), ALU.mult).then_inc(q_own[0], 1)
                    wait(dve, q_own, g, 2 * a + 2)
                    nc.vector.tensor_tensor(q_rot[:, :, 0:ROPE], q_rot[:, :, 0:ROPE], q_tmp,
                                            ALU.add).then_inc(q_rotated[0], 1)
                elif what == "S":
                    a, r = args
                    wait(dve, prev_copied, g, 4 * a + r + 1)
                    wait(dve, sub_done, g, 4 * a + r - 3)
                    scores = pair[:].rearrange("p b (h s n) -> p (b h) s n", h=2, s=2)
                    p4 = prob_of[a][:, HQ * r:HQ * r + HQ, :]
                    hold(dve)
                    nc.vector.copy_predicated(p4, seen_q[:].unsqueeze(1).broadcast_to([P, HQ, P]),
                                              scores[:, :, 1, :]).then_inc(s_merged[0], 1)
                    wait(dve, s_merged, g, 4 * a + r + 1)
                    nc.vector.tensor_reduce(top[:, HQ * r:HQ * r + HQ], p4, AX_X, ALU.max).then_inc(max_done[0], 1)
                elif what == "SUM":
                    a, r = args
                    wait(dve, exp_done, g, 4 * a + r + 1)
                    if r == 0:
                        wait(dve, recip_done, g, a - 1)
                    nc.vector.tensor_reduce(total_of[a][:, HQ * r:HQ * r + HQ], prob_of[a][:, HQ * r:HQ * r + HQ, :],
                                            AX_X, ALU.add).then_inc(sum_done[0], 1)
                elif what == "R":
                    a, = args
                    wait(dve, sum_done, g, 4 * a + 4)
                    wait(dve, rt_full, g, a)
                    nc.vector.reciprocal(recip[:], total_of[a][:]).then_inc(recip_own[0], 1)
                    wait(dve, recip_own, g, a + 1)
                    nc.vector.tensor_copy(recip_w[:], recip[:].rearrange("p (r c) -> p c r", c=HQ).unsqueeze(3)
                                          .broadcast_to([P, HQ, NQ, HD])).then_inc(recip_done[0], 1)
                elif what == "PT":
                    a, r = args
                    wait(dve, pt_hi_done, g, 4 * a + r + 1)
                    nc.vector.tensor_tensor(pt_lo[:, r % 2, :, :].rearrange("p h n -> p (h n)"), bank_c,
                                            pt_hi[:, r % 2, :, :].bitcast(F32).rearrange("p h n -> p (h n)"),
                                            ALU.subtract).then_inc(pt_split[0], 1)
                elif what == "PM":
                    a, r = args
                    wait(dve, pt_split, g, 4 * a + r + 1)
                    wait(dve, pv_done, g, 4 * a + r)
                    nc.vector.tensor_tensor(ptc_lo[:], pt_lo[:, r % 2, :, :].bitcast(F32),
                                            seen_k[:].unsqueeze(1).broadcast_to([P, HQ, P]),
                                            ALU.mult).then_inc(ptc_lo_done[0], 1)
                elif what == "O1":
                    a, = args
                    wait(dve, rt_copied, g, a + 1)
                    wait(dve, pv_done, g, 4 * a + 4)
                    nc.vector.tensor_tensor(o_f[:], bank_d, recip_t[:], ALU.mult).then_inc(o_scaled[0], 1)
                elif what == "O3":
                    a, = args
                    wait(dve, o_hi_done, g, a + 1)
                    nc.vector.tensor_tensor(o_lo[:], o_f[:], o_hi[:].bitcast(F32), ALU.subtract).then_inc(o_split[0], 1)
                elif what == "LN1":
                    a, = args
                    y = x1[:, par, a, :]
                    wait(dve, wo_full, g, a + 1)
                    wait(dve, xb_done, g, 1)
                    nc.vector.tensor_tensor(y, bank_c, y, ALU.add).then_inc(wo_added[0], 1)
                    wait(dve, wo_added, g, a + 1)
                    nc.vector.bn_stats(stats[:, a, :], y).then_inc(stats_own[0], 1)
                    wait(dve, stats_own, g, a + 1)
                    hold(dve)
                    nc.vector.bn_aggr(mean_var[:, a, :], stats[:, a, :]).then_inc(var_done[0], 1)
                elif what == "LN2":
                    a, = args
                    y = x1[:, par, a, :]
                    wait(dve, rstd_done, g, a + 1)
                    wait(dve, var_done, g, a + 1)
                    nc.vector.tensor_scalar(y, y, mean_var[:, a, 0:1], rstd[:, a:a + 1], ALU.subtract,
                                            ALU.mult).then_inc(x1_done[0], 1)
                elif what == "X1T":
                    wait(dve, x1t_hi_done, g, 1)
                    nc.vector.tensor_tensor(x1t_lo[:].rearrange("p c n -> p (c n)"),
                                            turned[:].rearrange("p b n -> p (b n)"),
                                            x1t_hi[:].bitcast(F32).rearrange("p c n -> p (c n)"),
                                            ALU.subtract).then_inc(x1t_split[0], 1)
                elif what == "A1":
                    i, = args
                    wait(dve, tanh_done, g, i + 1)
                    nc.vector.scalar_tensor_tensor(out=silu_t[:, i % 2, :], in0=tanh_t[:, i % 2, :], scalar=1.0,
                                                   in1=gu[:, i % 2, 0, :], op0=ALU.add, op1=ALU.mult).then_inc(silu_done[0], 1)
                elif what == "A2":
                    i, = args
                    wait(dve, silu_done, g, i + 1)
                    wait(dve, hid_split, g, i - 1)
                    nc.vector.scalar_tensor_tensor(out=hid_t[:, i % 2, :], in0=gu[:, i % 2, 1, :],
                                                   scalar=half_gu[:, i:i + 1], in1=silu_t[:, i % 2, :], op0=ALU.mult,
                                                   op1=ALU.mult).then_inc(hid_done[0], 1)
                elif what == "Y":
                    for a in range(TILES):
                        wait(dve, down_done, g, IC)
                        nc.vector.tensor_tensor(down_t[:, a, :], down[:, a, :], scale_d[:],
                                                ALU.mult).then_inc(down_read[0], 1)
                elif what == "YA":
                    for a in range(TILES):
                        y = x1[:, par, a, :]
                        wait(dve, down_read, g, a + 1)
                        wait(dve, x1_done, g, a + 1)
                        nc.vector.tensor_tensor(y, down_t[:, a, :], y, ALU.add).then_inc(y_added[0], 1)
                    for a in range(TILES):
                        wait(dve, y_added, g, a + 1)
                        nc.vector.bn_stats(stats2[:, a, :], x1[:, par, a, :]).then_inc(stats2_own[0], 1)
                    for a in range(TILES):
                        wait(dve, stats2_own, g, a + 1)
                        hold(dve)
                        nc.vector.bn_aggr(mean_var2[:, a, :], stats2[:, a, :]).then_inc(var2_done[0], 1)
                elif what == "YN":
                    for a in range(TILES):
                        y = x1[:, par, a, :]
                        wait(dve, rstd2_done, g, a + 1)
                        wait(dve, var2_done, g, a + 1)
                        nc.vector.tensor_scalar(y, y, mean_var2[:, a, 0:1], rstd2[:, a:a + 1], ALU.subtract,
                                                ALU.mult).then_inc(y_done[0], 1)

            for n, (hi, lo, src) in enumerate(attention_weights):
                dve.wait_ge(w_hi[0], n + 1)
                nc.vector.tensor_tensor(lo, src, hi.bitcast(F32), ALU.subtract).then_inc(w_lo[0], 1)
            dve.wait_ge(c_in[0], 16 * 7)
            nc.vector.tensor_copy(seen_q[:], mask_in).then_inc(seen_done[0], 1)
            dve.wait_ge(scales_t[0], 1)
            nc.vector.tensor_copy(scale_gu[:], gu[:, 0, 0, 0:2 * IC]).then_inc(scales_c[0], 1)
            dve.wait_ge(scales_c[0], 1)
            nc.vector.tensor_scalar(half_g[:], scale_gu[:, 0:IC], 0.5, None, ALU.mult).then_inc(scales_c[0], 1)
            dve.wait_ge(scales_c[0], 2)
            nc.vector.tensor_tensor(half_gu[:], half_g[:], scale_gu[:, IC:2 * IC], ALU.mult).then_inc(scales_c[0], 1)
            dve.wait_ge(scales_c[0], 3)
            dve.wait_ge(seen_done[0], 1)
            run(dve, order_of("vector"), step)

        @block.gpsimd
        def _(pool):
            def inverse_root(var, r, g, own, at, done):
                nc.gpsimd.tensor_tensor(r, var, eps[:], ALU.add).then_inc(own[0], 1)
                wait(pool, own, g, at)
                nc.gpsimd.tensor_tensor(r, r, minus_half[:], ALU.pow).then_inc(done[0], 1)

            def step(s, g):
                what, args = s[0], s[1:]
                reg, off = g
                par = off % 2
                if what == "W":
                    k, = args
                    if 1 <= k <= CHUNKS:
                        w, t = stage[:, (k - 1) % RING, 0, :], stage[:, (k - 1) % RING, 1, :]
                        pool.wait_ge(added[0], k)
                        nc.gpsimd.tensor_tensor(w, w, t, ALU.subtract).then_inc(taken[0], 1)
                elif what == "XB":
                    wait(pool, x_in, g, 32)
                    wait(pool, y_out, (reg, off - 1), 0)
                    if off == 1 and reg is None:
                        pool.wait_ge(seen_done[0], 1)
                        pool.wait_ge(scales_t[0], 1)
                    nc.gpsimd.tensor_tensor(x1[:, par, :, :], xin[:], bias_o[:].unsqueeze(1).broadcast_to([P, TILES, D]),
                                            ALU.add).then_inc(xb_done[0], 1)
                elif what == "KV":
                    wait(pool, kv_own, g, 3)
                    for a in range(TILES):
                        here = 2 * par + a
                        nc.gpsimd.tensor_tensor(vd[:, a, :], v_f[:, here, :], v_f[:, (here - 1) % 4, :],
                                                ALU.subtract)
                        nc.gpsimd.tensor_tensor(vd_hi[:, here, :], v_f[:, here, :], v_f[:, (here - 1) % 4, :],
                                                ALU.subtract).then_inc(vd_own[0], 1)
                    wait(pool, vd_own, g, 2)
                    nc.gpsimd.tensor_tensor(vd_lo[:, 2 * par:2 * par + 2, :], vd[:],
                                            vd_hi[:, 2 * par:2 * par + 2, :].bitcast(F32),
                                            ALU.subtract).then_inc(vd_split[0], 1)
                elif what == "QH":
                    a, = args
                    wait(pool, q_hi_done, g, a + 1)
                    nc.gpsimd.tensor_tensor(q_part_lo, q_rot.unsqueeze(2).broadcast_to([P, H, 2, HD]), q_part_hi,
                                            ALU.subtract).then_inc(q_split[0], 1)
                elif what == "S":
                    a, r = args
                    wait(pool, max_done, g, 4 * a + r + 1)
                    p4 = prob_of[a][:, HQ * r:HQ * r + HQ, :]
                    nc.gpsimd.tensor_tensor(p4, p4, top[:, HQ * r:HQ * r + HQ].unsqueeze(2).broadcast_to([P, HQ, P]),
                                            ALU.subtract).then_inc(sub_done[0], 1)
                elif what == "PM":
                    a, r = args
                    wait(pool, pv_done, g, 4 * a + r)
                    mask = seen_k[:].unsqueeze(1).broadcast_to([P, HQ, P])
                    wait(pool, pt_hi_done, g, 4 * a + r + 1)
                    nc.gpsimd.tensor_tensor(ptc_hi[:], pt_hi[:, r % 2, :, :].bitcast(F32), mask,
                                            ALU.mult).then_inc(pt_masked[0], 1)
                elif what == "LN1":
                    a, = args
                    wait(pool, var_done, g, a + 1)
                    inverse_root(mean_var[:, a, 1:2], rstd[:, a:a + 1], g, root_own, a + 1, rstd_done)
                elif what == "B":
                    i, = args
                    wait(pool, hid_hi_done, g, i + 1)
                    nc.gpsimd.tensor_tensor(hid_lo[:, i % HID, :], hid_t[:, i % 2, :], hid_hi[:, i % HID, :].bitcast(F32),
                                            ALU.subtract).then_inc(hid_split[0], 1)
                elif what == "Y":
                    for a in range(TILES):
                        wait(pool, var2_done, g, a + 1)
                        inverse_root(mean_var2[:, a, 1:2], rstd2[:, a:a + 1], g, root2_own, a + 1, rstd2_done)

            nc.gpsimd.memset(padded[:].bitcast(F32), 0.0)
            nc.gpsimd.memset(k_stack[:].bitcast(F32), 0.0)
            nc.gpsimd.memset(v_f[:], 0.0)
            nc.gpsimd.memset(round_min[:], -ROUND_MIN)
            nc.gpsimd.memset(eps[:], EPS)
            nc.gpsimd.memset(minus_half[:], -0.5).then_inc(zeroed[0], 1)
            pool.wait_ge(c_in[0], 16 * 7)
            pool.wait_ge(zeroed[0], 1)
            run(pool, order_of("gpsimd"), step)


_INS = ["L0_attn_x", "L0_attn_Wq", "L0_attn_Wk", "L0_attn_Wv", "L0_attn_Wo", "L0_attn_bo", "L0_ffn_gate_w",
        "L0_ffn_up_w", "L0_ffn_down_w", "L0_ffn_gate_scale", "L0_ffn_up_scale", "L0_ffn_down_scale"]


def constants(batch, length):
    half = ROPE // 2
    inv_freq = np.exp(-np.log(np.float32(10000.0)) * (np.arange(0, ROPE, 2, dtype=np.float32) / np.float32(ROPE)))
    theta = np.arange(length, dtype=np.float32)[:, None] * inv_freq.astype(np.float32)[None, :]
    rows = np.zeros((length, ROW), np.float32)
    rows[:, 0:half] = rows[:, half:ROPE] = np.cos(theta)
    rows[:, ROPE:HD] = 1.0
    rows[:, HD:HD + half] = -np.sin(theta)
    rows[:, HD + half:HD + ROPE] = np.sin(theta)
    rows[:P, ROW - 1] = NEG
    at = np.arange(P)
    seen = (at[:, None] <= at[None, :]).astype(np.float32)
    return np.tile(rows, (batch, 1)), np.eye(P, dtype=np.float32), np.stack([seen, seen.T.copy()])


def kernel(**inputs):
    import concourse.bacc as _bacc
    from concourse.bass_utils import run_bass_kernel_spmd as _run

    nc = _bacc.Bacc("TRN2", target_bir_lowering=False, num_devices=1, dynamic_dma_scratch_size=512)
    arrays, args = {}, []

    def give(name, a):
        arrays[name] = a
        args.append(nc.dram_tensor(name, a.shape, mybir.dt.from_np(a.dtype), kind="ExternalInput").ap())

    for name in _INS:
        a = np.ascontiguousarray(inputs[name])
        if name == "L0_attn_x":
            batch, length, width = a.shape
            a = a.reshape(batch * length, width)
        give(f"in_{name}", a)
    for name, a in zip(("rows", "ident", "seen"), constants(batch, length)):
        give(f"const_{name}", a)
    args.append(nc.dram_tensor("out_0", (batch * length, width), F32, kind="ExternalOutput").ap())
    layer_kernel(nc, *args)
    r = _run(nc, [arrays], core_ids=[0])
    return r.results[0]["out_0"].reshape(batch, length, width)
```

```python
from contextlib import ExitStack

import numpy as np

import concourse.bass as bass
from concourse import mybir

F32 = mybir.dt.float32
F32R = mybir.dt.float32r
I32 = mybir.dt.int32
U8 = mybir.dt.uint8
ALU = mybir.AluOpType
ACT = mybir.ActivationFunctionType
AX_X = mybir.AxisListType.X

P = 128
D = 512
H = 16
HD = 32
ROPE = HD // 2
DC = D // P
I = 1536
IC = I // P
TILES = 2
T = TILES * P
HQ = 4
NQ = H // HQ
SCALE = HD ** -0.5
EPS = 1e-5
NEG = -1e30
ROW = HD + ROPE + 1
PAD = 3 * HD

EXP_BITS = 0x7F800000
ROUND = 1.5 * 2.0 ** 20
ROUND_MIN = ROUND * 2.0 ** -6
OVER = float(np.float32(np.finfo(np.float32).max / 464))
OVER_BACK = float(np.float32(1.0 / np.float64(OVER)))
HID = 3
CHUNKS = 3 * IC
RING = 4
MAGICS = 2


ORDER = {
    "tensor": """
        PV.1.0:2 G.8:3 QT.0.0:1 PT.1.2:2 U.8:3 QT.0.1:1 QT.0.2:1 PV.1.1:2 DN.6:3 QT.0.3:1 G.9:3 PT.1.3:2 U.9:3
        S.0.0:1 PV.1.2:2 DN.7:3 S.0.1:1 G.10:3 PV.1.3:2 RT.1:2 S.0.2:1 U.10:3 DN.8:3 G.11:3 U.11:3 WO.1:2 S.0.3:1
        DN.9:3 X1T.0:2 DN.10:3 DN.11:3 PT.0.0:1 X1T.1:2 Q.1:1 PT.0.1:1 G.0:2 U.0:2 PV.0.0:1 G.1:2 PT.0.2:1 U.1:2
        G.2:2 QT.1.0:1 QT.1.1:1 U.2:2 QT.1.2:1 QT.1.3:1 PV.0.1:1 S.1.0:1 DN.0:2 G.3:2 PT.0.3:1 S.1.1:1 PV.0.2:1
        U.3:2 S.1.2:1 DN.1:2 G.4:2 U.4:2 S.1.3:1 DN.2:2 PV.0.3:1 RT.0:1 XT:0 G.5:2 U.5:2 DN.3:2 G.6:2 KV:0 WO.0:1
        KT:0 U.6:2 DN.4:2 Q.0:0 PT.1.0:1 G.7:2 U.7:2 DN.5:2 PT.1.1:1
    """,
    "vector": """
        R.0:2 A2.3:3 S.1.3:2 W.3:1 A1.4:3 W.22:2 A2.4:3 O1.0:2 XT:1 W.23:2 W.4:1 SUM.1.0:2 O3.0:2 A1.5:3 W.24:2
        KV:1 W.5:1 A2.5:3 KH:1 W.25:2 LN1.0:2 SUM.1.1:2 A1.6:3 W.6:1 W.7:1 W.26:2 Q.0:1 W.8:1 PT.1.0:2 W.0:0
        PM.1.0:2 A2.6:3 SUM.1.2:2 W.27:2 PT.1.1:2 W.1:0 A1.7:3 SUM.1.3:2 SW.3:1 PM.1.1:2 W.9:1 W.10:1 W.28:2
        PT.1.2:2 A2.7:3 LNS.0:2 W.29:2 PM.1.2:2 R.1:2 PT.1.3:2 W.30:2 A1.8:3 A2.8:3 S.0.0:1 PM.1.3:2 W.11:1
        A1.9:3 A2.9:3 W.31:2 S.0.1:1 W.32:2 W.12:1 O1.1:2 SUM.0.0:1 O3.1:2 W.33:2 A1.10:3 A2.10:3 S.0.2:1 A1.11:3
        A2.11:3 LN2.0:2 W.34:2 LN1.1:2 LNS.1:2 W.13:1 W.35:2 X1T.0:2 LN2.1:2 S.0.3:1 W.14:1 Y.0:3 W.36:2 X1T.1:2
        PT.0.0:1 Y.1:3 W.37:2 PM.0.0:1 W.15:1 Q.1:1 PT.0.1:1 YA.0:3 YA.1:3 A1.0:2 A2.0:2 PM.0.1:1 YS.0:3 A1.1:2
        W.16:1 W.17:1 YS.1:3 PT.0.2:1 W.2:0 SUM.0.1:1 A2.1:2 YN.0:3 SW.2:0 W.18:1 YN.1:3 PM.0.2:1 SUM.0.2:1
        S.1.0:1 W.19:1 A1.2:2 SUM.0.3:1 S.1.1:1 A2.2:2 PT.0.3:1 W.20:1 S.1.2:1 PM.0.3:1 A1.3:2 W.21:1
    """,
    "scalar": """
        PT.0.0:2 W.2:1 E.0.1:2 W.14:2 PT.0.1:2 E.0.2:2 A1.0:3 QH.1:2 A1.1:3 W.15:2 W.16:2 PT.0.2:2 B.0:3 QT.1.0:2
        QT.1.1:2 E.0.3:2 W.17:2 QT.1.2:2 QT.1.3:2 A1.2:3 B.1:3 W.0:0 S.1.0:2 W.18:2 PT.0.3:2 S.1.1:2 W.19:2
        A1.3:3 S.1.2:2 W.20:2 B.2:3 A1.4:3 S.1.3:2 B.3:3 E.1.0:2 W.21:2 RT.0:2 XT:1 E.1.1:2 W.22:2 W.3:1 E.1.2:2
        O2.0:2 A1.5:3 W.4:1 W.23:2 SW.3:1 W.24:2 KV:1 KH:1 B.4:3 A1.6:3 W.25:2 W.5:1 KT:1 B.5:3 W.6:1 W.7:1
        PT.1.0:2 E.1.3:2 QH.0:1 W.26:2 A1.7:3 PT.1.1:2 W.8:1 B.6:3 W.27:2 QT.0.0:1 PT.1.2:2 QT.0.1:1 QT.0.2:1
        W.28:2 A1.8:3 QT.0.3:1 PT.1.3:2 B.7:3 A1.9:3 W.9:1 W.29:2 S.0.0:1 W.10:1 W.30:2 S.0.1:1 W.31:2 B.8:3
        E.0.0:1 RT.1:2 W.11:1 A1.10:3 O2.1:2 W.32:2 S.0.2:1 B.9:3 A1.11:3 W.1:0 W.33:2 B.10:3 W.34:2 SW.2:0
        W.12:1 B.11:3 X1T.0:2 S.0.3:1 W.35:2 W.13:1 X1T.1:2
    """,
    "gpsimd": """
        W.17:2 W.18:2 PM.0.2:2 B.1:3 XB:2 W.1:0 W.19:2 B.2:3 PM.0.3:2 W.5:1 W.20:2 S.1.0:2 S.1.1:2 W.21:2 W.22:2
        S.1.2:2 W.23:2 B.3:3 S.1.3:2 B.4:3 W.24:2 W.2:0 W.25:2 KV:1 B.5:3 W.3:0 W.26:2 W.6:1 PM.1.0:2 W.4:0 W.7:1
        QH.0:1 W.27:2 PM.1.1:2 W.28:2 W.8:1 W.9:1 B.6:3 PM.1.2:2 W.29:2 W.30:2 B.7:3 PM.1.3:2 W.10:1 S.0.0:1
        W.31:2 W.11:1 B.8:3 W.32:2 W.12:1 LNS.0:2 S.0.1:1 B.9:3 W.13:1 W.33:2 B.10:3 S.0.2:1 W.14:1 B.11:3 W.34:2
        LNS.1:2 W.35:2 W.36:2 PM.0.0:1 S.0.3:1 W.15:1 QH.1:1 W.16:1 PM.0.1:1 B.0:2 YS.0:3 YS.1:3
    """,
    "sync": """
        C.18:2 C.26:3 C.27:3 C.4:0 C.5:0 C.10:1 C.11:1 C.12:1 C.28:3 C.19:2 C.13:1 C.29:3 C.14:1 C.6:0 C.30:3
        C.31:3 C.32:3 C.33:3 C.34:3 C.20:2 C.35:3 C.15:1 C.21:2 C.7:0 C.22:2 LD:1 C.8:0 C.23:2 C.24:2 ST:3 C.16:1
        C.25:2 C.17:1 C.9:0
    """,
}


def order_of(engine):
    steps = []
    for word in ORDER[engine].split():
        name, age = word.split(":")
        name, *at = name.split(".")
        steps.append((int(age), (name, *map(int, at))))
    return steps


ONCE = ("C", "W", "SW")
AGES = 1 + max(age for engine in ORDER for age, _ in order_of(engine))


def layer_kernel(nc, x, wq, wk, wv, wo, bo, gate_w, up_w, down_w, gate_s, up_s, down_s, rows, ident_d, seen_d, out):
    TOKENS = x.shape[0]
    GROUPS = TOKENS // T
    BEFORE = AGES + 1
    PAIRS = (GROUPS - BEFORE) // 2
    assert TOKENS % T == 0 and PAIRS > 0 and x.shape[1] == D

    with ExitStack() as ctx:
        def sb(name, shape, dt=F32):
            return ctx.enter_context(nc.sbuf_tensor(name, shape, dt))

        pair = ctx.enter_context(nc.psum_tensor("pair", [P, 2, 512], F32))
        turned = ctx.enter_context(nc.psum_tensor("turned", [P, 2, 512], F32))
        bank_a, bank_b, bank_c, bank_d = pair[:, 0, :], pair[:, 1, :], turned[:, 0, :], turned[:, 1, :]
        gu = ctx.enter_context(nc.psum_tensor("gu", [P, 2, 2, T], F32))
        down = ctx.enter_context(nc.psum_tensor("down", [P, TILES, D], F32))

        wq_hi, wq_lo = sb("wq_hi", [P, DC, D], F32R), sb("wq_lo", [P, DC, D], F32R)
        wkv = sb("wkv", [P, DC, 2, 2 * HD], F32R)
        wkv_hi, wkv_lo = wkv[:, :, 0, :], wkv[:, :, 1, :]
        wo_hi, wo_lo = sb("wo_hi", [P, HQ, D], F32R), sb("wo_lo", [P, HQ, D], F32R)
        gate_q, up_q = sb("gate_q", [P, IC, DC, P], F32R), sb("up_q", [P, IC, DC, P], F32R)
        down_q = sb("down_q", [P, IC, D], F32R)
        ident = sb("ident", [P, P])
        seen_k = sb("seen_k", [P, P])
        seen_q = sb("seen_q", [P, P], U8)
        bias_o = sb("bias_o", [P, D])
        scale_d = sb("scale_d", [P, D])
        scale_gu = sb("scale_gu", [P, 2 * IC])
        half_g = sb("half_g", [P, IC])
        half_gu = sb("half_gu", [P, IC])
        minus_half = sb("minus_half", [P, 1])
        eps = sb("eps", [P, 1])
        round_min = sb("round_min", [P, 1])
        stage = sb("stage", [P, RING + MAGICS, 512])
        magic = stage[:, RING:, :]
        mlp_tmp = stage[:].rearrange("p r n -> p (r n)")
        tanh_t = mlp_tmp[:, 0:2 * T].rearrange("p (b n) -> p b n", b=2)
        silu_t = mlp_tmp[:, 2 * T:4 * T].rearrange("p (b n) -> p b n", b=2)
        hid_t = mlp_tmp[:, 4 * T:6 * T].rearrange("p (b n) -> p b n", b=2)
        down_t = mlp_tmp[:, 6 * T:6 * T + TILES * D].rearrange("p (a n) -> p a n", a=TILES)
        xin = sb("xin", [P, TILES, D])
        pos = sb("pos", [P, 2, TILES, ROW])
        x1 = sb("x1", [P, 2, TILES, D])
        mask_in = x1[:, 1, 0, 0:P]
        scale_in = x1[0:2 * IC, 1, 1, 0:P]
        xt_hi, xt_lo = sb("xt_hi", [P, DC, T], F32R), sb("xt_lo", [P, DC, T], F32R)
        x1t_hi, x1t_lo = sb("x1t_hi", [P, DC, T], F32R), sb("x1t_lo", [P, DC, T], F32R)
        q_part = sb("q_part", [P, H, 4, HD])
        q_rot = q_part[:, :, 3, :]
        q_tmp = q_part[:, :, 1, 0:ROPE]
        q_part_hi = q_part[:].rearrange("p h (u v) n -> p h u v n", v=2)[:, :, :, 0, :]
        q_part_lo = q_part[:].rearrange("p h (u v) n -> p h u v n", v=2)[:, :, :, 1, :]
        q_stack = sb("q_stack", [P, H, P], F32R)
        k_part = sb("k_part", [P, TILES, 4, HD])
        k_rot = k_part[:, :, 3, :]
        k_tmp = k_part[:, :, 1, 0:ROPE]
        k_stack = sb("k_stack", [P, 4, P], F32R)
        kv_f = sb("kv_f", [P, 4, 2 * HD])
        v_f = kv_f[:, :, HD:]
        vd = sb("vd", [P, TILES, HD])
        padded = sb("padded", [P, PAD + 16 * P], F32R)
        values = padded[:, PAD:].rearrange("p (s n) -> p s n", n=P)[:, :, 0:HD]
        v_hi, v_lo, vd_hi, vd_lo = values[:, 0:4, :], values[:, 4:8, :], values[:, 8:12, :], values[:, 12:16, :]
        prob_of = [sb(f"prob{a}", [P, H, P]) for a in range(TILES)]
        top = sb("top", [P, H])
        total_of = [sb(f"total{a}", [P, H]) for a in range(TILES)]
        recip = sb("recip", [P, H])
        recip_w = sb("recip_w", [P, HQ, NQ, HD])
        pt_hi, pt_lo = sb("pt_hi", [P, 2, HQ, P], F32R), sb("pt_lo", [P, 2, HQ, P], F32R)
        ptc_hi, ptc_lo = sb("ptc_hi", [P, HQ, P], F32R), sb("ptc_lo", [P, HQ, P], F32R)
        recip_t = sb("recip_t", [P, HQ * P])
        o_f = recip_t
        o_hi, o_lo = sb("o_hi", [P, HQ * P], F32R), sb("o_lo", [P, HQ * P], F32R)
        hid_hi, hid_lo = sb("hid_hi", [P, HID, T], F32R), sb("hid_lo", [P, HID, T], F32R)
        stats, mean_var, rstd = sb("stats", [P, TILES, 6]), sb("mean_var", [P, TILES, 2]), sb("rstd", [P, TILES])
        stats2, mean_var2, rstd2 = sb("stats2", [P, TILES, 6]), sb("mean_var2", [P, TILES, 2]), sb("rstd2", [P, TILES])

        def signal(name, per=1):
            return ctx.enter_context(nc.semaphore(name)), per

        def wait(eng, sig, g, k):
            sem, per = sig
            reg, off = g
            at = off * per + k
            if reg is not None:
                assert at > 0
                eng.wait_ge(sem, reg * (2 * per) + at)
            elif at > 0:
                eng.wait_ge(sem, at)

        passed = ctx.enter_context(nc.semaphore("passed"))

        def hold(eng):
            eng.sem_inc(passed, 1)

        x_in = signal("x_in", 32)
        w_in = [signal(f"w_in_{n}") for n in ("k", "v", "q", "o")]
        ident_in = signal("ident_in")
        scale_gu_in = signal("scale_gu_in")
        seen_in = signal("seen_in")
        c_in = signal("c_in")
        chunk_in = [signal(f"chunk_in{s}") for s in range(RING)]
        y_out = [signal(f"y_out{parity}") for parity in range(2)]
        zeroed = signal("zeroed")
        w_hi = signal("w_hi")
        w_lo = signal("w_lo")
        seen_done = signal("seen_done")
        scales_t = signal("scales_t")
        scales_c = signal("scales_c")
        expo_done = signal("expo_done")
        magic_a, magic_done = signal("magic_a"), signal("magic_done")
        added = signal("added")
        taken = signal("taken")
        quantised = signal("quantised")
        xt_full = signal("xt_full")
        kv_full = signal("kv_full")
        q_full = signal("q_full", 2)
        kt_full = signal("kt_full")
        qt_full = signal("qt_full", 8)
        s_full = signal("s_full", 8)
        pt_full = signal("pt_full", 8)
        pv_done = signal("pv_done", 8)
        rt_full = signal("rt_full", 2)
        wo_full = signal("wo_full", 2)
        x1t_full = signal("x1t_full", 2)
        xt_hi_done = signal("xt_hi_done")
        xt_split = signal("xt_split")
        xb_done = signal("xb_done")
        v_hi_done = signal("v_hi_done")
        k_hi_done = signal("k_hi_done")
        k_rotated = signal("k_rotated")
        kv_read = signal("kv_read")
        k_split = signal("k_split")
        vd_split = signal("vd_split")
        kt_copied = signal("kt_copied")
        q_rotated = signal("q_rotated", 2)
        q_hi_done = signal("q_hi_done", 2)
        q_split = signal("q_split", 2)
        qt_copied = signal("qt_copied", 8)
        prev_copied = signal("prev_copied", 8)
        s_merged = signal("s_merged", 8)
        max_done = signal("max_done", 8)
        sub_done = signal("sub_done", 8)
        exp_done = signal("exp_done", 8)
        sum_done = signal("sum_done", 8)
        recip_done = signal("recip_done", 2)
        pt_hi_done = signal("pt_hi_done", 8)
        pt_split = signal("pt_split", 8)
        pt_masked = signal("pt_masked", 8)
        rt_copied = signal("rt_copied", 2)
        o_scaled = signal("o_scaled", 2)
        o_hi_done = signal("o_hi_done", 2)
        o_split = signal("o_split", 2)
        wo_added = signal("wo_added", 2)
        var_done = signal("var_done", 2)
        rstd_done = signal("rstd_done", 2)
        x1_done = signal("x1_done", 2)
        x1t_hi_done = signal("x1t_hi_done", 2)
        x1t_split = signal("x1t_split", 2)
        gu_full = signal("gu_full", IC)
        tanh_done = signal("tanh_done", IC)
        silu_done = signal("silu_done", IC)
        hid_done = signal("hid_done", IC)
        hid_hi_done = signal("hid_hi_done", IC)
        hid_split = signal("hid_split", IC)
        down_done = signal("down_done", IC)
        down_read = signal("down_read", 2)
        y_added = signal("y_added", 2)
        var2_done = signal("var2_done", 2)
        rstd2_done = signal("rstd2_done", 2)
        y_done = signal("y_done", 2)
        kv_own = signal("kv_own", 3)
        q_own = signal("q_own", 4)
        recip_own = signal("recip_own", 2)
        stats_own = signal("stats_own", 2)
        stats2_own = signal("stats2_own", 2)
        vd_own = signal("vd_own", 2)
        root_own = signal("root_own", 2)
        root2_own = signal("root2_own", 2)
        ptc_lo_done = signal("ptc_lo_done", 8)

        block = ctx.enter_context(nc.Block())

        def run(eng, order, step):
            def peeled(n):
                for age, s in order:
                    if 0 <= n - age < (1 if s[0] in ONCE else GROUPS):
                        step(s, (None, n - age))

            for n in range(BEFORE):
                peeled(n)
            with eng.Fori(0, PAIRS) as j:
                for n in (BEFORE, BEFORE + 1):
                    for age, s in order:
                        if s[0] not in ONCE:
                            step(s, (j, n - age))
            for n in range(BEFORE + 2 * PAIRS, GROUPS + AGES - 1):
                peeled(n)

        def chunk_src(k):
            i, kind = divmod(k, 3)
            if kind == 2:
                return down_w[i * P:(i + 1) * P, :]
            w = (gate_w, up_w)[kind]
            return w.rearrange("(c p) n -> p c n", p=P)[:, :, i * P:(i + 1) * P]

        def chunk_dst(k):
            i, kind = divmod(k, 3)
            return down_q[:, i, :] if kind == 2 else (gate_q, up_q)[kind][:, i, :, :].rearrange("p c n -> p (c n)")

        wk_stage = recip_t[:, 0:DC * HD].rearrange("p (c n) -> p c n", c=DC)
        wv_stage = recip_t[:, DC * HD:2 * DC * HD].rearrange("p (c n) -> p c n", c=DC)
        wq_stage = prob_of[0][:].rearrange("p h n -> p (h n)").rearrange("p (c n) -> p c n", c=DC)
        wo_stage = prob_of[1][:].rearrange("p h n -> p (h n)").rearrange("p (c n) -> p c n", c=HQ)
        attention_weights = [(wkv_hi[:, :, 0:HD], wkv_lo[:, :, 0:HD], wk_stage), (wkv_hi[:, :, HD:], wkv_lo[:, :, HD:], wv_stage),
                             (wq_hi[:], wq_lo[:], wq_stage), (wo_hi[:], wo_lo[:], wo_stage)]

        @block.sync
        def _(sp):
            x_t = x.rearrange("(t p) d -> p t d", p=P)
            rows_t = rows.rearrange("(t p) d -> p t d", p=P)
            out_t = out.rearrange("(t p) d -> p t d", p=P)

            def load_x(g):
                reg, off = g
                wait(sp, xt_full, g, 0)
                hold(sp)
                wait(sp, xb_done, g, 0)
                hold(sp)
                wait(sp, q_rotated, (reg, off - 1), 0)
                hold(sp)
                wait(sp, prev_copied, (reg, off - 1), 0)
                hold(sp)
                first = off * TILES if reg is None else reg * (2 * TILES) + off * TILES
                ts = bass.ds(first, TILES)
                sp.dma_start(xin[:], x_t[:, ts, :]).then_inc(x_in[0], 16)
                sp.dma_start(pos[:, off % 2, :, :], rows_t[:, ts, :]).then_inc(x_in[0], 16)

            def load_chunk(k):
                if k >= RING:
                    sp.wait_ge(quantised[0], k - RING + 1)
                dst = stage[:, k % RING, :]
                sp.dma_start(dst if k % 3 == 2 else dst.rearrange("p (c n) -> p c n", c=DC),
                             chunk_src(k)).then_inc(chunk_in[k % RING][0], 16)

            def step(s, g):
                if s[0] == "ST":
                    store_y(g)
                elif s[0] == "C":
                    load_chunk(*s[1:])
                elif g[0] is not None or g[1] > 0:
                    load_x(g)

            sp.dma_start(ident[:], ident_d).then_inc(ident_in[0], 16)
            load_x((None, 0))
            sp.dma_start(seen_k[:], seen_d[0]).then_inc(seen_in[0], 16)
            sp.dma_start(mask_in, seen_d[1]).then_inc(seen_in[0], 16)
            sp.dma_start(scale_in[0:IC], gate_s.rearrange("(i p) -> i p", p=P)).then_inc(scale_gu_in[0], 16)
            sp.dma_start(scale_in[IC:2 * IC], up_s.rearrange("(i p) -> i p", p=P)).then_inc(scale_gu_in[0], 16)
            for n, (dst, src) in enumerate(((wk_stage, wk), (wv_stage, wv), (wq_stage, wq))):
                sp.dma_start(dst, src.rearrange("(c p) n -> p c n", p=P)).then_inc(w_in[n][0], 16)
            for k in range(RING):
                load_chunk(k)
            for r in range(NQ):
                sp.dma_start(wo_stage[r * HD:(r + 1) * HD, :, :],
                             wo[r * P:(r + 1) * P, :].rearrange("(c d) n -> d c n", d=HD)).then_inc(w_in[3][0], 16)
            sp.dma_start(bias_o[:], bo.partition_broadcast(P)).then_inc(c_in[0], 16)
            sp.dma_start(scale_d[:], down_s.partition_broadcast(P)).then_inc(c_in[0], 16)

            def store_y(g):
                reg, off = g
                wait(sp, y_done, g, 2)
                hold(sp)
                first = off * TILES if reg is None else reg * (2 * TILES) + off * TILES
                sp.dma_start(out_t[:, bass.ds(first, TILES), :], x1[:, off % 2, :, :]).then_inc(y_out[off % 2][0], 16)

            run(sp, order_of("sync"), step)
            sp.wait_ge(y_out[0][0], 16 * ((GROUPS + 1) // 2))
            sp.wait_ge(y_out[1][0], 16 * (GROUPS // 2))

        @block.tensor
        def _(pe):
            def split_product(bank, lhs_hi, lhs_lo, rhs_hi, rhs_lo, n):
                for c in range(n):
                    nc.tensor.matmul(bank, lhs_hi(c), rhs_hi(c), start=(c == 0), stop=False)
                    nc.tensor.matmul(bank, lhs_hi(c), rhs_lo(c), start=False, stop=False)
                    last = nc.tensor.matmul(bank, lhs_lo(c), rhs_hi(c), start=False, stop=(c == n - 1))
                return last

            def step(s, g):
                what, args = s[0], s[1:]
                reg, off = g
                par = off % 2
                if what == "XT":
                    wait(pe, x_in, g, 32)
                    wait(pe, s_merged, g, 0)
                    for c in range(DC):
                        for a in range(TILES):
                            col = (c % 2) * T + a * P
                            last = nc.tensor.transpose(pair[:, c // 2, col:col + P],
                                                       xin[:, a, c * P:(c + 1) * P], ident[:])
                    last.then_inc(xt_full[0], 1)
                elif what == "KV":
                    if off == 0 and reg is None:
                        pe.wait_ge(w_lo[0], 2)
                        pe.wait_ge(w_hi[0], 2)
                    wait(pe, xt_split, g, 1)
                    for a in range(TILES):
                        at = a * 4 * HD
                        for c in range(DC):
                            nc.tensor.matmul(bank_a[:, at:at + 4 * HD], xt_hi[:, c, a * P:(a + 1) * P],
                                             wkv[:, c, :, :].rearrange("p u n -> p (u n)"), start=(c == 0), stop=False)
                            last = nc.tensor.matmul(bank_a[:, at:at + 2 * HD], xt_lo[:, c, a * P:(a + 1) * P],
                                                    wkv[:, c, 0, :], start=False, stop=(c == DC - 1))
                    last.then_inc(kv_full[0], 1)
                elif what == "Q":
                    a, = args
                    if off == 0 and reg is None and a == 0:
                        pe.wait_ge(w_lo[0], 3)
                    if a == 0:
                        wait(pe, kv_read, g, 1)
                        wait(pe, k_split, g, 1)
                    else:
                        wait(pe, s_merged, g, 4)
                    split_product(bank_a, lambda c: xt_hi[:, c, a * P:(a + 1) * P],
                                  lambda c: xt_lo[:, c, a * P:(a + 1) * P],
                                  lambda c: wq_hi[:, c, :], lambda c: wq_lo[:, c, :], DC).then_inc(q_full[0], 1)
                elif what == "KT":
                    wait(pe, k_split, g, 1)
                    for a in range(TILES):
                        last = nc.tensor.transpose(bank_b[:, a * P:(a + 1) * P],
                                                   k_part[:, a, :, :].rearrange("p u n -> p (u n)"), ident[:])
                    last.then_inc(kt_full[0], 1)
                elif what == "QT":
                    a, r = args
                    wait(pe, q_split, g, a + 1)
                    if r == 0 and a == 0:
                        wait(pe, kt_copied, g, 1)
                    elif r >= 2:
                        wait(pe, qt_copied, g, 4 * a + r - 1)
                    bank = bank_a if r % 2 else bank_b
                    for n in range(HQ):
                        last = nc.tensor.transpose(bank[:, n * P:(n + 1) * P],
                                                   q_part[:, HQ * r + n, :, :].rearrange("p u n -> p (u n)"), ident[:])
                    last.then_inc(qt_full[0], 1)
                elif what == "S":
                    a, r = args
                    if r == 0:
                        wait(pe, qt_copied, g, 4 * a + 4)
                    else:
                        wait(pe, s_merged, g, 4 * a + r)
                    slot = 2 * par + a
                    keys = k_stack[:, slot - 1:slot + 1, :] if slot else k_stack[:, 3::-3, :]
                    for n in range(HQ):
                        last = nc.tensor.matmul(pair[:, n // 2, (n % 2) * 2 * P:(n % 2 + 1) * 2 * P],
                                                q_stack[:, HQ * r + n, :], keys, start=True, stop=True)
                    last.then_inc(s_full[0], 1)
                elif what == "PT":
                    a, r = args
                    wait(pe, exp_done, g, 4 * a + r + 1)
                    if r > 0:
                        wait(pe, pt_split, g, 4 * a + r)
                    elif a == 0:
                        wait(pe, x1t_split, g, -1)
                    else:
                        wait(pe, wo_added, g, 1)
                    for n in range(HQ):
                        last = nc.tensor.transpose(bank_c[:, n * P:(n + 1) * P],
                                                   prob_of[a][:, HQ * r + n, :], ident[:])
                    last.then_inc(pt_full[0], 1)
                elif what == "PV":
                    a, r = args
                    wait(pe, pt_split, g, 4 * a + r + 1)
                    wait(pe, pt_masked, g, 4 * a + r + 1)
                    wait(pe, ptc_lo_done, g, 4 * a + r + 1)
                    if r == 0 and a == 0:
                        wait(pe, vd_split, g, 1)
                        wait(pe, x1t_split, g, 0)
                    elif r == 0:
                        wait(pe, o_scaled, g, 1)
                    prev = (2 * par + a - 1) % 4

                    def window(slot):
                        return padded[:, slot * P + PAD - HD * r:slot * P + PAD - HD * r + P]

                    hi, lo = pt_hi[:, r % 2, :, :], pt_lo[:, r % 2, :, :]
                    here = 2 * par + a
                    pairs = [(window(prev), hi), (window(4 + prev), hi), (window(prev), lo), (window(8 + here), ptc_hi[:]),
                             (window(12 + here), ptc_hi[:]), (window(8 + here), ptc_lo[:])]
                    for n, (v, p) in enumerate(pairs):
                        last = nc.tensor.matmul(bank_d, v, p, start=(r == 0 and n == 0), stop=(r == NQ - 1 and n == 5))
                    last.then_inc(pv_done[0], 1)
                elif what == "RT":
                    a, = args
                    wait(pe, recip_done, g, a + 1)
                    for c in range(HQ):
                        last = nc.tensor.transpose(bank_c[:, c * P:(c + 1) * P],
                                                   recip_w[:, c, :, :].rearrange("p r n -> p (r n)"), ident[:])
                    last.then_inc(rt_full[0], 1)
                elif what == "WO":
                    a, = args
                    if off == 0 and reg is None and a == 0:
                        pe.wait_ge(w_lo[0], 4)
                    wait(pe, o_split, g, a + 1)
                    split_product(bank_c, lambda c: o_hi[:, c * P:(c + 1) * P], lambda c: o_lo[:, c * P:(c + 1) * P],
                                  lambda c: wo_hi[:, c, :], lambda c: wo_lo[:, c, :], HQ).then_inc(wo_full[0], 1)
                elif what == "X1T":
                    a, = args
                    wait(pe, x1_done, g, a + 1)
                    if a == 0:
                        wait(pe, wo_added, g, 2)
                    else:
                        wait(pe, o_scaled, g, 2)
                    for c in range(DC):
                        last = nc.tensor.transpose(turned[:, a, c * P:(c + 1) * P],
                                                   x1[:, par, a, c * P:(c + 1) * P], ident[:])
                    last.then_inc(x1t_full[0], 1)
                elif what in ("G", "U"):
                    i, = args
                    u = int(what == "U")
                    if off == 0 and reg is None and i == 0 and u == 0:
                        pe.wait_ge(quantised[0], CHUNKS)
                    if i == 0 and u == 0:
                        wait(pe, x1t_split, g, 2)
                    if u == 0:
                        wait(pe, hid_done, g, i - 1)
                    w = (gate_q, up_q)[u]
                    for c in range(DC):
                        nc.tensor.matmul(gu[:, i % 2, u, :], w[:, i, c, :], x1t_hi[:, c, :], start=(c == 0), stop=False)
                        last = nc.tensor.matmul(gu[:, i % 2, u, :], w[:, i, c, :], x1t_lo[:, c, :], start=False,
                                                stop=(c == DC - 1))
                    if u:
                        last.then_inc(gu_full[0], 1)
                elif what == "DN":
                    i, = args
                    wait(pe, hid_split, g, i + 1)
                    if i == 0:
                        wait(pe, down_read, g, 0)
                    for a in range(TILES):
                        for n, part in enumerate((hid_hi, hid_lo)):
                            last = nc.tensor.matmul(down[:, a, :], part[:, i % HID, a * P:(a + 1) * P], down_q[:, i, :],
                                                    start=(i == 0 and n == 0), stop=(i == IC - 1 and n == 1))
                    last.then_inc(down_done[0], 1)

            pe.wait_ge(ident_in[0], 16)
            pe.wait_ge(scale_gu_in[0], 16 * 2)
            nc.tensor.transpose(gu[:, 0, 0, 0:2 * IC], scale_in, ident[0:2 * IC, 0:2 * IC]).then_inc(scales_t[0], 1)
            run(pe, order_of("tensor"), step)

        @block.scalar
        def _(act):
            def step(s, g):
                what, args = s[0], s[1:]
                reg, off = g
                par = off % 2
                if what == "W":
                    k, = args
                    if k < CHUNKS:
                        t = magic[:, k % MAGICS, :]
                        act.wait_ge(expo_done[0], k + 1)
                        nc.scalar.activation(t, t, ACT.Relu, bias=round_min[:], scale=ROUND).then_inc(magic_a[0], 1)
                        act.wait_ge(magic_a[0], k + 1)
                        nc.scalar.activation(t, t, ACT.Copy, bias=ROUND_MIN).then_inc(magic_done[0], 1)
                elif what == "SW":
                    n, = args
                    hi, _, src = attention_weights[n]
                    act.wait_ge(w_in[n][0], 64 if n == 3 else 16)
                    nc.scalar.activation(hi, src, ACT.Copy).then_inc(w_hi[0], 1)
                elif what == "XT":
                    wait(act, xt_full, g, 1)
                    wait(act, q_full, g, 0)
                    nc.scalar.activation(xt_hi[:].rearrange("p c n -> p (c n)"),
                                         pair[:].rearrange("p b n -> p (b n)"), ACT.Copy).then_inc(xt_hi_done[0], 1)
                elif what == "KV":
                    wait(act, kv_read, g, 1)
                    wait(act, pv_done, g, -4)
                    nc.scalar.activation(v_hi[:, 2 * par:2 * par + 2, :], v_f[:, 2 * par:2 * par + 2, :],
                                         ACT.Copy).then_inc(v_hi_done[0], 1)
                elif what == "KH":
                    wait(act, k_rotated, g, 1)
                    nc.scalar.activation(k_part[:, :, 0:2, :].bitcast(F32R),
                                         k_rot.unsqueeze(2).broadcast_to([P, TILES, 2, HD]), ACT.Copy).then_inc(k_hi_done[0], 1)
                elif what == "QH":
                    a, = args
                    wait(act, q_rotated, g, a + 1)
                    nc.scalar.activation(q_part_hi.bitcast(F32R), q_rot.unsqueeze(2).broadcast_to([P, H, 2, HD]),
                                         ACT.Copy).then_inc(q_hi_done[0], 1)
                elif what == "KT":
                    wait(act, kt_full, g, 1)
                    nc.scalar.activation(k_stack[:, 2 * par:2 * par + 2, :],
                                         bank_b[:, 0:TILES * P].rearrange("p (a n) -> p a n", a=TILES),
                                         ACT.Copy).then_inc(kt_copied[0], 1)
                elif what == "QT":
                    a, r = args
                    wait(act, qt_full, g, 4 * a + r + 1)
                    nc.scalar.activation(q_stack[:, HQ * r:HQ * r + HQ, :],
                                         (bank_a if r % 2 else bank_b).rearrange("p (h n) -> p h n", h=HQ),
                                         ACT.Copy).then_inc(qt_copied[0], 1)
                elif what == "S":
                    a, r = args
                    if off == 0 and reg is None and a == 1 and r == 0:
                        act.wait_ge(w_lo[0], 4)
                    wait(act, s_full, g, 4 * a + r + 1)
                    wait(act, sum_done, g, 4 * a + r - 7)
                    wait(act, pt_full, g, 4 * a + r - 7)
                    scores = pair[:].rearrange("p b (h s n) -> p (b h) s n", h=2, s=2)
                    nc.scalar.activation(prob_of[a][:, HQ * r:HQ * r + HQ, :], scores[:, :, 0, :], ACT.Identity,
                                         bias=pos[:, par, a, ROW - 1:ROW]).then_inc(prev_copied[0], 1)
                elif what == "E":
                    a, r = args
                    wait(act, sub_done, g, 4 * a + r + 1)
                    q4 = prob_of[a][:, HQ * r:HQ * r + HQ, :].rearrange("p h n -> p (h n)")
                    nc.scalar.activation(q4, q4, ACT.Exp, scale=SCALE).then_inc(exp_done[0], 1)
                elif what == "PT":
                    a, r = args
                    wait(act, pt_full, g, 4 * a + r + 1)
                    wait(act, pv_done, g, 4 * a + r - 1)
                    nc.scalar.activation(pt_hi[:, r % 2, :, :].rearrange("p h n -> p (h n)"), bank_c,
                                         ACT.Copy).then_inc(pt_hi_done[0], 1)
                elif what == "RT":
                    a, = args
                    wait(act, rt_full, g, a + 1)
                    wait(act, o_split, g, a)
                    nc.scalar.activation(recip_t[:], bank_c, ACT.Copy).then_inc(rt_copied[0], 1)
                elif what == "O2":
                    a, = args
                    wait(act, o_scaled, g, a + 1)
                    wait(act, wo_full, g, a)
                    nc.scalar.activation(o_hi[:], o_f[:], ACT.Copy).then_inc(o_hi_done[0], 1)
                elif what == "X1T":
                    a, = args
                    wait(act, x1t_full, g, a + 1)
                    wait(act, gu_full, g, 0)
                    nc.scalar.activation(x1t_hi[:, :, a * P:(a + 1) * P],
                                         turned[:, a, :].rearrange("p (c n) -> p c n", c=DC),
                                         ACT.Copy).then_inc(x1t_hi_done[0], 1)
                elif what == "A1":
                    i, = args
                    if off == 0 and reg is None and i == 0:
                        act.wait_ge(scales_c[0], 3)
                    wait(act, gu_full, g, i + 1)
                    wait(act, silu_done, g, i - 1)
                    nc.scalar.activation(tanh_t[:, i % 2, :], gu[:, i % 2, 0, :], ACT.Tanh,
                                         scale=half_g[:, i:i + 1]).then_inc(tanh_done[0], 1)
                elif what == "B":
                    i, = args
                    wait(act, hid_done, g, i + 1)
                    wait(act, down_done, g, i + 1 - HID)
                    nc.scalar.activation(hid_hi[:, i % HID, :], hid_t[:, i % 2, :], ACT.Copy).then_inc(hid_hi_done[0], 1)

            step(("SW", 0), (None, 0))
            step(("SW", 1), (None, 0))
            act.wait_ge(zeroed[0], 1)
            run(act, order_of("scalar"), step)

        @block.vector
        def _(dve):
            def step(s, g):
                what, args = s[0], s[1:]
                reg, off = g
                par = off % 2
                if what == "W":
                    k, = args
                    if k >= 2:
                        w = stage[:, (k - 2) % RING, :]
                        dve.wait_ge(taken[0], k - 1)
                        nc.vector.tensor_scalar(chunk_dst(k - 2), w, OVER, OVER_BACK, ALU.mult,
                                                ALU.mult).then_inc(quantised[0], 1)
                    if k < CHUNKS:
                        w, t = stage[:, k % RING, :], magic[:, k % MAGICS, :]
                        dve.wait_ge(chunk_in[k % RING][0], 16 * (k // RING + 1))
                        nc.vector.tensor_scalar(t.bitcast(I32), w.bitcast(I32), EXP_BITS, None,
                                                ALU.bitwise_and).then_inc(expo_done[0], 1)
                    if 1 <= k <= CHUNKS:
                        w, t = stage[:, (k - 1) % RING, :], magic[:, (k - 1) % MAGICS, :]
                        dve.wait_ge(magic_done[0], k)
                        nc.vector.tensor_tensor(w, w, t, ALU.add).then_inc(added[0], 1)
                elif what == "SW":
                    n, = args
                    hi, lo, src = attention_weights[n]
                    dve.wait_ge(w_hi[0], n + 1)
                    nc.vector.tensor_tensor(lo, src, hi.bitcast(F32), ALU.subtract).then_inc(w_lo[0], 1)
                elif what == "XT":
                    wait(dve, xt_hi_done, g, 1)
                    nc.vector.tensor_tensor(xt_lo[:].rearrange("p c n -> p (c n)"),
                                            pair[:].rearrange("p b n -> p (b n)"),
                                            xt_hi[:].bitcast(F32).rearrange("p c n -> p (c n)"),
                                            ALU.subtract).then_inc(xt_split[0], 1)
                elif what == "KV":
                    wait(dve, x_in, g, 32)
                    wait(dve, kv_full, g, 1)
                    wait(dve, vd_split, g, 0)
                    parts = bank_a[:, 0:TILES * 4 * HD].rearrange("p (a u n) -> p a u n", a=TILES, u=2)
                    kv = kv_f[:, 2 * par:2 * par + 2, :]
                    nc.vector.tensor_copy(kv, parts[:, :, 1, :]).then_inc(kv_own[0], 1)
                    wait(dve, kv_own, g, 1)
                    nc.vector.tensor_tensor(kv, parts[:, :, 0, :], kv, ALU.add).then_inc(kv_read[0], 1)
                    cos, sin = pos[:, par, :, 0:HD], pos[:, par, :, HD:HD + ROPE]
                    wait(dve, kv_read, g, 1)
                    nc.vector.tensor_tensor(k_rot, kv[:, :, 0:HD], cos, ALU.mult).then_inc(kv_own[0], 1)
                    swapped = kv[:, :, 0:ROPE].rearrange("p a (u e) -> p a u e", u=2)[:, :, ::-1, :]
                    nc.vector.tensor_tensor(k_tmp.rearrange("p a (u e) -> p a u e", u=2), swapped,
                                            sin.rearrange("p a (u e) -> p a u e", u=2), ALU.mult).then_inc(kv_own[0], 1)
                    wait(dve, kv_own, g, 3)
                    nc.vector.tensor_tensor(k_rot[:, :, 0:ROPE], k_rot[:, :, 0:ROPE], k_tmp,
                                            ALU.add).then_inc(k_rotated[0], 1)
                elif what == "KH":
                    wait(dve, k_hi_done, g, 1)
                    nc.vector.tensor_tensor(k_part[:, :, 2:4, :], k_rot.unsqueeze(2).broadcast_to([P, TILES, 2, HD]),
                                            k_part[:, :, 0:2, :], ALU.subtract).then_inc(k_split[0], 1)
                elif what == "Q":
                    a, = args
                    wait(dve, q_full, g, a + 1)
                    wait(dve, q_split, g, a)
                    cos, sin = pos[:, par, a, 0:HD], pos[:, par, a, HD:HD + ROPE]
                    q3 = bank_a.rearrange("p (h n) -> p h n", h=H)
                    nc.vector.tensor_tensor(q_rot, q3, cos.unsqueeze(1).broadcast_to([P, H, HD]),
                                            ALU.mult).then_inc(q_own[0], 1)
                    swapped = q3[:, :, 0:ROPE].rearrange("p h (u e) -> p h u e", u=2)[:, :, ::-1, :]
                    nc.vector.tensor_tensor(q_tmp.rearrange("p h (u e) -> p h u e", u=2), swapped,
                                            sin.rearrange("p (u e) -> p u e", u=2).unsqueeze(1)
                                            .broadcast_to([P, H, 2, ROPE // 2]), ALU.mult).then_inc(q_own[0], 1)
                    wait(dve, q_own, g, 2 * a + 2)
                    nc.vector.tensor_tensor(q_rot[:, :, 0:ROPE], q_rot[:, :, 0:ROPE], q_tmp,
                                            ALU.add).then_inc(q_rotated[0], 1)
                elif what == "S":
                    a, r = args
                    wait(dve, prev_copied, g, 4 * a + r + 1)
                    wait(dve, sub_done, g, 4 * a + r - 3)
                    scores = pair[:].rearrange("p b (h s n) -> p (b h) s n", h=2, s=2)
                    p4 = prob_of[a][:, HQ * r:HQ * r + HQ, :]
                    hold(dve)
                    nc.vector.copy_predicated(p4, seen_q[:].unsqueeze(1).broadcast_to([P, HQ, P]),
                                              scores[:, :, 1, :]).then_inc(s_merged[0], 1)
                    wait(dve, s_merged, g, 4 * a + r + 1)
                    nc.vector.tensor_reduce(top[:, HQ * r:HQ * r + HQ], p4, AX_X, ALU.max).then_inc(max_done[0], 1)
                elif what == "SUM":
                    a, r = args
                    wait(dve, exp_done, g, 4 * a + r + 1)
                    if r == 0:
                        wait(dve, recip_done, g, a - 1)
                    nc.vector.tensor_reduce(total_of[a][:, HQ * r:HQ * r + HQ], prob_of[a][:, HQ * r:HQ * r + HQ, :],
                                            AX_X, ALU.add).then_inc(sum_done[0], 1)
                elif what == "R":
                    a, = args
                    wait(dve, sum_done, g, 4 * a + 4)
                    wait(dve, rt_full, g, a)
                    nc.vector.reciprocal(recip[:], total_of[a][:]).then_inc(recip_own[0], 1)
                    wait(dve, recip_own, g, a + 1)
                    nc.vector.tensor_copy(recip_w[:], recip[:].rearrange("p (r c) -> p c r", c=HQ).unsqueeze(3)
                                          .broadcast_to([P, HQ, NQ, HD])).then_inc(recip_done[0], 1)
                elif what == "PT":
                    a, r = args
                    wait(dve, pt_hi_done, g, 4 * a + r + 1)
                    nc.vector.tensor_tensor(pt_lo[:, r % 2, :, :].rearrange("p h n -> p (h n)"), bank_c,
                                            pt_hi[:, r % 2, :, :].bitcast(F32).rearrange("p h n -> p (h n)"),
                                            ALU.subtract).then_inc(pt_split[0], 1)
                elif what == "PM":
                    a, r = args
                    wait(dve, pt_split, g, 4 * a + r + 1)
                    wait(dve, pv_done, g, 4 * a + r)
                    nc.vector.tensor_tensor(ptc_lo[:], pt_lo[:, r % 2, :, :].bitcast(F32),
                                            seen_k[:].unsqueeze(1).broadcast_to([P, HQ, P]),
                                            ALU.mult).then_inc(ptc_lo_done[0], 1)
                elif what == "O1":
                    a, = args
                    wait(dve, rt_copied, g, a + 1)
                    wait(dve, pv_done, g, 4 * a + 4)
                    nc.vector.tensor_tensor(o_f[:], bank_d, recip_t[:], ALU.mult).then_inc(o_scaled[0], 1)
                elif what == "O3":
                    a, = args
                    wait(dve, o_hi_done, g, a + 1)
                    nc.vector.tensor_tensor(o_lo[:], o_f[:], o_hi[:].bitcast(F32), ALU.subtract).then_inc(o_split[0], 1)
                elif what == "LN1":
                    a, = args
                    y = x1[:, par, a, :]
                    wait(dve, wo_full, g, a + 1)
                    wait(dve, xb_done, g, 1)
                    nc.vector.tensor_tensor(y, bank_c, y, ALU.add).then_inc(wo_added[0], 1)
                elif what == "LNS":
                    a, = args
                    y = x1[:, par, a, :]
                    wait(dve, wo_added, g, a + 1)
                    nc.vector.bn_stats(stats[:, a, :], y).then_inc(stats_own[0], 1)
                    wait(dve, stats_own, g, a + 1)
                    hold(dve)
                    nc.vector.bn_aggr(mean_var[:, a, :], stats[:, a, :]).then_inc(var_done[0], 1)
                elif what == "LN2":
                    a, = args
                    y = x1[:, par, a, :]
                    wait(dve, rstd_done, g, a + 1)
                    wait(dve, var_done, g, a + 1)
                    nc.vector.tensor_scalar(y, y, mean_var[:, a, 0:1], rstd[:, a:a + 1], ALU.subtract,
                                            ALU.mult).then_inc(x1_done[0], 1)
                elif what == "X1T":
                    a, = args
                    wait(dve, x1t_hi_done, g, a + 1)
                    nc.vector.tensor_tensor(x1t_lo[:, :, a * P:(a + 1) * P],
                                            turned[:, a, :].rearrange("p (c n) -> p c n", c=DC),
                                            x1t_hi[:, :, a * P:(a + 1) * P].bitcast(F32),
                                            ALU.subtract).then_inc(x1t_split[0], 1)
                elif what == "A1":
                    i, = args
                    wait(dve, tanh_done, g, i + 1)
                    nc.vector.scalar_tensor_tensor(out=silu_t[:, i % 2, :], in0=tanh_t[:, i % 2, :], scalar=1.0,
                                                   in1=gu[:, i % 2, 0, :], op0=ALU.add, op1=ALU.mult).then_inc(silu_done[0], 1)
                elif what == "A2":
                    i, = args
                    wait(dve, silu_done, g, i + 1)
                    wait(dve, hid_split, g, i - 1)
                    nc.vector.scalar_tensor_tensor(out=hid_t[:, i % 2, :], in0=gu[:, i % 2, 1, :],
                                                   scalar=half_gu[:, i:i + 1], in1=silu_t[:, i % 2, :], op0=ALU.mult,
                                                   op1=ALU.mult).then_inc(hid_done[0], 1)
                elif what == "Y":
                    a, = args
                    if off == 0 and reg is None:
                        dve.wait_ge(c_in[0], 16 * 2)
                    wait(dve, down_done, g, IC)
                    nc.vector.tensor_tensor(down_t[:, a, :], down[:, a, :], scale_d[:], ALU.mult).then_inc(down_read[0], 1)
                elif what == "YA":
                    a, = args
                    y = x1[:, par, a, :]
                    wait(dve, down_read, g, a + 1)
                    wait(dve, x1_done, g, a + 1)
                    nc.vector.tensor_tensor(y, down_t[:, a, :], y, ALU.add).then_inc(y_added[0], 1)
                elif what == "YS":
                    a, = args
                    wait(dve, y_added, g, a + 1)
                    nc.vector.bn_stats(stats2[:, a, :], x1[:, par, a, :]).then_inc(stats2_own[0], 1)
                    wait(dve, stats2_own, g, a + 1)
                    hold(dve)
                    nc.vector.bn_aggr(mean_var2[:, a, :], stats2[:, a, :]).then_inc(var2_done[0], 1)
                elif what == "YN":
                    a, = args
                    y = x1[:, par, a, :]
                    wait(dve, rstd2_done, g, a + 1)
                    wait(dve, var2_done, g, a + 1)
                    nc.vector.tensor_scalar(y, y, mean_var2[:, a, 0:1], rstd2[:, a:a + 1], ALU.subtract,
                                            ALU.mult).then_inc(y_done[0], 1)

            step(("SW", 0), (None, 0))
            step(("SW", 1), (None, 0))
            dve.wait_ge(seen_in[0], 16 * 2)
            nc.vector.tensor_copy(seen_q[:], mask_in).then_inc(seen_done[0], 1)
            dve.wait_ge(scales_t[0], 1)
            nc.vector.tensor_copy(scale_gu[:], gu[:, 0, 0, 0:2 * IC]).then_inc(scales_c[0], 1)
            dve.wait_ge(scales_c[0], 1)
            nc.vector.tensor_scalar(half_g[:], scale_gu[:, 0:IC], 0.5, None, ALU.mult).then_inc(scales_c[0], 1)
            dve.wait_ge(scales_c[0], 2)
            nc.vector.tensor_tensor(half_gu[:], half_g[:], scale_gu[:, IC:2 * IC], ALU.mult).then_inc(scales_c[0], 1)
            dve.wait_ge(scales_c[0], 3)
            dve.wait_ge(seen_done[0], 1)
            run(dve, order_of("vector"), step)

        @block.gpsimd
        def _(pool):
            def inverse_root(var, r, g, own, at, done):
                nc.gpsimd.tensor_tensor(r, var, eps[:], ALU.add).then_inc(own[0], 1)
                wait(pool, own, g, at)
                nc.gpsimd.tensor_tensor(r, r, minus_half[:], ALU.pow).then_inc(done[0], 1)

            def step(s, g):
                what, args = s[0], s[1:]
                reg, off = g
                par = off % 2
                if what == "W":
                    k, = args
                    if 1 <= k <= CHUNKS:
                        w, t = stage[:, (k - 1) % RING, :], magic[:, (k - 1) % MAGICS, :]
                        pool.wait_ge(added[0], k)
                        nc.gpsimd.tensor_tensor(w, w, t, ALU.subtract).then_inc(taken[0], 1)
                elif what == "XB":
                    if off == 0 and reg is None:
                        pool.wait_ge(c_in[0], 16 * 2)
                    wait(pool, x_in, g, 32)
                    if reg is not None:
                        pool.wait_ge(y_out[par][0], reg * 16 + off // 2 * 16)
                    elif off >= 2:
                        pool.wait_ge(y_out[par][0], off // 2 * 16)
                    if off == 1 and reg is None:
                        pool.wait_ge(seen_done[0], 1)
                        pool.wait_ge(scales_t[0], 1)
                    nc.gpsimd.tensor_tensor(x1[:, par, :, :], xin[:], bias_o[:].unsqueeze(1).broadcast_to([P, TILES, D]),
                                            ALU.add).then_inc(xb_done[0], 1)
                elif what == "KV":
                    wait(pool, v_hi_done, g, 1)
                    nc.gpsimd.tensor_tensor(v_lo[:, 2 * par:2 * par + 2, :], v_f[:, 2 * par:2 * par + 2, :],
                                            v_hi[:, 2 * par:2 * par + 2, :].bitcast(F32), ALU.subtract)
                    for a in range(TILES):
                        here = 2 * par + a
                        nc.gpsimd.tensor_tensor(vd[:, a, :], v_f[:, here, :], v_f[:, (here - 1) % 4, :],
                                                ALU.subtract)
                        nc.gpsimd.tensor_tensor(vd_hi[:, here, :], v_f[:, here, :], v_f[:, (here - 1) % 4, :],
                                                ALU.subtract).then_inc(vd_own[0], 1)
                    wait(pool, vd_own, g, 2)
                    nc.gpsimd.tensor_tensor(vd_lo[:, 2 * par:2 * par + 2, :], vd[:],
                                            vd_hi[:, 2 * par:2 * par + 2, :].bitcast(F32),
                                            ALU.subtract).then_inc(vd_split[0], 1)
                elif what == "QH":
                    a, = args
                    wait(pool, q_hi_done, g, a + 1)
                    nc.gpsimd.tensor_tensor(q_part_lo, q_rot.unsqueeze(2).broadcast_to([P, H, 2, HD]), q_part_hi,
                                            ALU.subtract).then_inc(q_split[0], 1)
                elif what == "S":
                    a, r = args
                    wait(pool, max_done, g, 4 * a + r + 1)
                    p4 = prob_of[a][:, HQ * r:HQ * r + HQ, :]
                    nc.gpsimd.tensor_tensor(p4, p4, top[:, HQ * r:HQ * r + HQ].unsqueeze(2).broadcast_to([P, HQ, P]),
                                            ALU.subtract).then_inc(sub_done[0], 1)
                elif what == "PM":
                    a, r = args
                    wait(pool, pv_done, g, 4 * a + r)
                    mask = seen_k[:].unsqueeze(1).broadcast_to([P, HQ, P])
                    wait(pool, pt_hi_done, g, 4 * a + r + 1)
                    nc.gpsimd.tensor_tensor(ptc_hi[:], pt_hi[:, r % 2, :, :].bitcast(F32), mask,
                                            ALU.mult).then_inc(pt_masked[0], 1)
                elif what == "LNS":
                    a, = args
                    wait(pool, var_done, g, a + 1)
                    inverse_root(mean_var[:, a, 1:2], rstd[:, a:a + 1], g, root_own, a + 1, rstd_done)
                elif what == "B":
                    i, = args
                    wait(pool, hid_hi_done, g, i + 1)
                    nc.gpsimd.tensor_tensor(hid_lo[:, i % HID, :], hid_t[:, i % 2, :], hid_hi[:, i % HID, :].bitcast(F32),
                                            ALU.subtract).then_inc(hid_split[0], 1)
                elif what == "YS":
                    a, = args
                    wait(pool, var2_done, g, a + 1)
                    inverse_root(mean_var2[:, a, 1:2], rstd2[:, a:a + 1], g, root2_own, a + 1, rstd2_done)

            nc.gpsimd.memset(padded[:].bitcast(F32), 0.0)
            nc.gpsimd.memset(k_stack[:].bitcast(F32), 0.0)
            nc.gpsimd.memset(v_f[:], 0.0)
            nc.gpsimd.memset(round_min[:], -ROUND_MIN)
            nc.gpsimd.memset(eps[:], EPS)
            nc.gpsimd.memset(minus_half[:], -0.5).then_inc(zeroed[0], 1)
            pool.wait_ge(seen_in[0], 16 * 2)
            pool.wait_ge(zeroed[0], 1)
            run(pool, order_of("gpsimd"), step)


_INS = ["L0_attn_x", "L0_attn_Wq", "L0_attn_Wk", "L0_attn_Wv", "L0_attn_Wo", "L0_attn_bo", "L0_ffn_gate_w",
        "L0_ffn_up_w", "L0_ffn_down_w", "L0_ffn_gate_scale", "L0_ffn_up_scale", "L0_ffn_down_scale"]


def constants(batch, length):
    half = ROPE // 2
    inv_freq = np.exp(-np.log(np.float32(10000.0)) * (np.arange(0, ROPE, 2, dtype=np.float32) / np.float32(ROPE)))
    theta = np.arange(length, dtype=np.float32)[:, None] * inv_freq.astype(np.float32)[None, :]
    rows = np.zeros((length, ROW), np.float32)
    rows[:, 0:half] = rows[:, half:ROPE] = np.cos(theta)
    rows[:, ROPE:HD] = 1.0
    rows[:, HD:HD + half] = -np.sin(theta)
    rows[:, HD + half:HD + ROPE] = np.sin(theta)
    rows[:P, ROW - 1] = NEG
    at = np.arange(P)
    seen = (at[:, None] <= at[None, :]).astype(np.float32)
    return np.tile(rows, (batch, 1)), np.eye(P, dtype=np.float32), np.stack([seen, seen.T.copy()])


def kernel(**inputs):
    import concourse.bacc as _bacc
    from concourse.bass_utils import run_bass_kernel_spmd as _run

    nc = _bacc.Bacc("TRN2", target_bir_lowering=False, num_devices=1, dynamic_dma_scratch_size=512)
    arrays, args = {}, []

    def give(name, a):
        arrays[name] = a
        args.append(nc.dram_tensor(name, a.shape, mybir.dt.from_np(a.dtype), kind="ExternalInput").ap())

    for name in _INS:
        a = np.ascontiguousarray(inputs[name])
        if name == "L0_attn_x":
            batch, length, width = a.shape
            a = a.reshape(batch * length, width)
        give(f"in_{name}", a)
    for name, a in zip(("rows", "ident", "seen"), constants(batch, length)):
        give(f"const_{name}", a)
    args.append(nc.dram_tensor("out_0", (batch * length, width), F32, kind="ExternalOutput").ap())
    layer_kernel(nc, *args)
    r = _run(nc, [arrays], core_ids=[0])
    return r.results[0]["out_0"].reshape(batch, length, width)
```
